# Optimizing a Trainium2 kernel written in Bass

```python
import numpy as np
import jax
import jax.numpy as jnp

def _softmax(x, axis=-1):
    return jax.nn.softmax(x, axis=axis)

def _gelu(x):
    return jax.nn.gelu(x, approximate=True)

def _silu(x):
    return jax.nn.silu(x)

def _sigmoid(x):
    return jax.nn.sigmoid(x)

def _layernorm(x, axis=-1, eps=1e-05):
    m = jnp.mean(x, axis=axis, keepdims=True)
    v = jnp.var(x, axis=axis, keepdims=True)
    return (x - m) / jnp.sqrt(v + eps)

def _scatter_add(tgt, idx, src, axis=0):
    return tgt.at[idx].add(src)

def _segment_sum(src, seg, n):
    return jax.ops.segment_sum(src, seg, n)
kernel_name = 'mk_prb_d1_jaxref_r4_b132f3'

def setup_inputs(seed: int=0):
    np.random.seed(seed)
    _w = jnp.asarray

    def _L0_attn_setup():
        import jax, jax.numpy as jnp
        import numpy as np
        B, S, HID = (4, 1024, 256)
        H, D = (16, 64)
        EPS = 1e-06

        def _phi(x):
            return jax.nn.elu(x) + 1.0
        key = jax.random.key(seed)
        ks = jax.random.split(key, 9)
        sc = 1.0 / np.sqrt(HID)
        return {'x': jax.random.normal(ks[0], (B, S, HID), jnp.float32), 'Wq': jax.random.normal(ks[1], (HID, H * D), jnp.float32) * sc, 'bq': jnp.zeros((H * D,), jnp.float32), 'Wk': jax.random.normal(ks[2], (HID, H * D), jnp.float32) * sc, 'bk': jnp.zeros((H * D,), jnp.float32), 'Wv': jax.random.normal(ks[3], (HID, H * D), jnp.float32) * sc, 'bv': jnp.zeros((H * D,), jnp.float32), 'Wo': jax.random.normal(ks[4], (H * D, HID), jnp.float32) * sc, 'bo': jnp.zeros((HID,), jnp.float32)}
    _L0_attn_in = _L0_attn_setup()

    def _L0_ffn_setup():
        import jax, jax.numpy as jnp
        import numpy as np
        D_MODEL = 256
        DEPTH = 8
        M = 2 ** DEPTH
        N_INTERNAL = M - 1
        B, T = (8, 1024)

        def _leaf_probs(gate):
            BT = gate.shape[0]
            lp = jnp.ones((BT, M), dtype=gate.dtype)
            for level in range(DEPTH):
                n = 2 ** level
                half = M // (2 * n)
                g = gate[:, n - 1:2 * n - 1]
                f = jnp.stack([1.0 - g, g], axis=-1)
                f = jnp.broadcast_to(f[..., None], (BT, n, 2, half))
                lp = lp * f.reshape(BT, M)
            return lp
        key = jax.random.key(seed)
        ks = jax.random.split(key, 7)
        x = jax.random.normal(ks[0], (B, T, D_MODEL), dtype=jnp.float32)
        Wq = jax.random.normal(ks[1], (D_MODEL, D_MODEL), dtype=jnp.float32) * 0.02
        routers = jax.random.normal(ks[2], (N_INTERNAL, D_MODEL), dtype=jnp.float32) * 0.02
        leaf_keys = jax.random.normal(ks[3], (M, D_MODEL), dtype=jnp.float32) * 0.02
        leaf_values = jax.random.normal(ks[4], (M, D_MODEL), dtype=jnp.float32) * 0.02
        Wout_w = jax.random.normal(ks[5], (D_MODEL, D_MODEL), dtype=jnp.float32) * 0.02
        Wout_b = jax.random.normal(ks[6], (D_MODEL,), dtype=jnp.float32) * 0.02
        return {'x': x, 'Wq': Wq, 'routers': routers, 'leaf_keys': leaf_keys, 'leaf_values': leaf_values, 'Wout_w': Wout_w, 'Wout_b': Wout_b}
    _L0_ffn_in = _L0_ffn_setup()
    _d = {'L0_attn_x': _L0_attn_in['x'], 'L0_attn_Wq': _L0_attn_in['Wq'], 'L0_attn_bq': _L0_attn_in['bq'], 'L0_attn_Wk': _L0_attn_in['Wk'], 'L0_attn_bk': _L0_attn_in['bk'], 'L0_attn_Wv': _L0_attn_in['Wv'], 'L0_attn_bv': _L0_attn_in['bv'], 'L0_attn_Wo': _L0_attn_in['Wo'], 'L0_attn_bo': _L0_attn_in['bo'], 'L0_ffn_Wq': _L0_ffn_in['Wq'], 'L0_ffn_routers': _L0_ffn_in['routers'], 'L0_ffn_leaf_keys': _L0_ffn_in['leaf_keys'], 'L0_ffn_leaf_values': _L0_ffn_in['leaf_values'], 'L0_ffn_Wout_w': _L0_ffn_in['Wout_w'], 'L0_ffn_Wout_b': _L0_ffn_in['Wout_b']}
    _x0 = _d['L0_attn_x']
    _d['L0_attn_x'] = jax.random.normal(jax.random.fold_in(jax.random.key(seed), 1), (4, 2048, 256), dtype=_x0.dtype)
    del _x0
    return _d

def reference(L0_attn_x, L0_attn_Wq, L0_attn_bq, L0_attn_Wk, L0_attn_bk, L0_attn_Wv, L0_attn_bv, L0_attn_Wo, L0_attn_bo, L0_ffn_Wq, L0_ffn_routers, L0_ffn_leaf_keys, L0_ffn_leaf_values, L0_ffn_Wout_w, L0_ffn_Wout_b):

    def _L0_attn_ref(x, Wq, bq, Wk, bk, Wv, bv, Wo, bo):
        import jax, jax.numpy as jnp
        import numpy as np
        B, S, HID = (4, 1024, 256)
        H, D = (16, 64)
        EPS = 1e-06

        def _phi(x):
            return jax.nn.elu(x) + 1.0
        bs, n, _ = x.shape
        Q = _phi((x @ Wq + bq).reshape(bs, n, H, D)).transpose(1, 0, 2, 3)
        K = _phi((x @ Wk + bk).reshape(bs, n, H, D)).transpose(1, 0, 2, 3)
        V = (x @ Wv + bv).reshape(bs, n, H, D).transpose(1, 0, 2, 3)
        KV0 = jnp.zeros((bs, H, D, D), x.dtype)
        Ks0 = jnp.zeros((bs, H, D), x.dtype)

        def step(carry, qkv):
            KV, Ks = carry
            qi, ki, vi = qkv
            KV = KV + jnp.einsum('bhd,bhe->bhde', ki, vi)
            Ks = Ks + ki
            num = jnp.einsum('bhd,bhde->bhe', qi, KV)
            den = jnp.einsum('bhd,bhd->bh', qi, Ks)
            return ((KV, Ks), num / (den[..., None] + EPS))
        _, out = jax.lax.scan(step, (KV0, Ks0), (Q, K, V))
        out = out.transpose(1, 0, 2, 3).reshape(bs, n, H * D)
        return out @ Wo + bo

    def _L0_ffn_ref(x, Wq, routers, leaf_keys, leaf_values, Wout_w, Wout_b):
        import jax, jax.numpy as jnp
        import numpy as np
        D_MODEL = 256
        DEPTH = 8
        M = 2 ** DEPTH
        N_INTERNAL = M - 1
        B, T = (8, 1024)

        def _leaf_probs(gate):
            BT = gate.shape[0]
            lp = jnp.ones((BT, M), dtype=gate.dtype)
            for level in range(DEPTH):
                n = 2 ** level
                half = M // (2 * n)
                g = gate[:, n - 1:2 * n - 1]
                f = jnp.stack([1.0 - g, g], axis=-1)
                f = jnp.broadcast_to(f[..., None], (BT, n, 2, half))
                lp = lp * f.reshape(BT, M)
            return lp
        Bv, Tv, d = x.shape
        q = jnp.einsum('btd,ed->bte', x, Wq)
        q_flat = q.reshape(Bv * Tv, d)
        gate = jax.nn.sigmoid(q_flat @ routers.T)
        leaf_prob = _leaf_probs(gate)
        ret = (leaf_prob @ leaf_values).reshape(Bv, Tv, d)
        return jnp.einsum('btd,ed->bte', ret, Wout_w) + Wout_b
    x = L0_attn_x
    xn = _layernorm(x, axis=-1)
    x = x + _L0_attn_ref(xn, L0_attn_Wq, L0_attn_bq, L0_attn_Wk, L0_attn_bk, L0_attn_Wv, L0_attn_bv, L0_attn_Wo, L0_attn_bo) + _L0_ffn_ref(xn, L0_ffn_Wq, L0_ffn_routers, L0_ffn_leaf_keys, L0_ffn_leaf_values, L0_ffn_Wout_w, L0_ffn_Wout_b)
    return x

_drawn_inputs = setup_inputs


def setup_inputs(seed=0):
    import zlib

    import numpy as np

    out = dict(_drawn_inputs(seed))
    spreads = {'L0_attn_bq': (0.0, 0.8),
     'L0_attn_bk': (0.0, 0.8),
     'L0_attn_bv': (0.0, 0.1),
     'L0_attn_bo': (0.0, 0.1)}
    factors = {'L0_attn_Wq': 6.16,
     'L0_attn_Wk': 3.405,
     'L0_ffn_Wq': 8.0,
     'L0_ffn_routers': 8.0,
     'L0_ffn_leaf_values': 8.0,
     'L0_ffn_Wout_w': 8.0,
     'L0_ffn_Wout_b': 2.793}
    for name, (base, spread) in spreads.items():
        noise = np.random.default_rng([zlib.crc32(name.encode()), seed]).standard_normal(out[name].shape)
        drawn = base * np.exp(spread * noise) if base else spread * noise
        out[name] = jnp.asarray(drawn.astype(out[name].dtype))
    for name, factor in factors.items():
        out[name] = (out[name] * factor).astype(out[name].dtype)
    return out
```

```python
from contextlib import ExitStack

import concourse.bass as bass
from concourse import mybir

ALU = mybir.AluOpType
ACT = mybir.ActivationFunctionType
F32 = mybir.dt.float32
F32R = mybir.dt.float32r

P = 128
HEADS, D = 16, 64
PAIRS = HEADS // 2
TOK = 512
CH = TOK // P
AUG = D + 1
HALF = PAIRS // 2
EPS_ATTN = 1e-6
EPS_NORM = 1e-5
AHEAD = 1

FIRST_FILLS = (["xnT0", "xnT1"] + [f"V0c{c}" for c in range(CH)] + ["K0", "Q0", "gate0", "gate1"]
               + ["tree_out0", "tree_out1"])
FILLS = []
for _p in range(PAIRS - 1):
    FILLS += [f"K{_p + 1}", f"Q{_p + 1}"]
    if _p < CH:
        FILLS.append(f"V1c{_p}")
    elif _p < CH + 2:
        FILLS.append(f"leafT{_p - CH}")
FILLS += ["xnT0", "xnT1"] + [f"V0c{c}" for c in range(CH)] + ["K0", "Q0", "gate0", "gate1", "y0", "y1"]
PER_BANK = len(FILLS) // 2
FIRST_PER_BANK = len(FIRST_FILLS) // 2
assert len(FILLS) % 2 == 0 and len(FIRST_FILLS) % 2 == 0


def bank_of(name):
    return FILLS.index(name) % 2


def count_of(name, g):
    return g * PER_BANK + (FIRST_PER_BANK + FILLS.index(name) // 2 + 1)


def count_before(name, g):
    return g * PER_BANK + (FIRST_PER_BANK + FILLS.index(name) // 2 + 1 - PER_BANK)


def first_count(name):
    return FIRST_FILLS.index(name) // 2 + 1


def attention_and_tree_layer(nc, x, Wq, bq, Wk, bk, Wv, bv, Wo, bo,
                             tree_Wq, routers, leaf_keys, leaf_values, Wout_w, Wout_b, out):
    batches, seq, hid = x.shape
    KT_ = hid // P
    MACROS = seq // TOK
    inner = HEADS * D
    leaves = leaf_values.shape[0]
    nodes = routers.shape[0]
    depth = leaves.bit_length() - 1
    LT = leaves // P
    assert KT_ == 2 and LT == 2 and nodes == leaves - 1 and Wq.shape[1] == inner

    x_rows = x.rearrange("b (t c p) d -> (b t) p c d", c=CH, p=P)
    out_rows = out.rearrange("b (t c p) d -> (b t) p c d", c=CH, p=P)

    with ExitStack() as ctx:
        def sb(name, shape, dt=F32):
            return ctx.enter_context(nc.sbuf_tensor(name, shape, dt))

        def sem(name):
            return ctx.enter_context(nc.semaphore(name))

        wq = sb("wq", [P, 2, KT_, inner], F32R)
        wk = sb("wk", [P, 2, KT_, inner], F32R)
        wv = sb("wv", [P, 2, KT_, inner], F32R)
        wo = sb("wo", [P, 2, PAIRS, hid], F32R)
        route = sb("route", [P, 2, KT_, leaves], F32R)
        tree_w = sb("tree_w", [P, 2, LT, hid], F32R)

        ident = sb("ident", [P, P])
        bias_rows = sb("bias_rows", [2 * PAIRS, P])
        neg_bias = sb("neg_bias", [P, 2 * PAIRS])
        bias_one = sb("bias_one", [P, 2 * PAIRS])
        bv_all = sb("bv_all", [P, inner])
        y_bias = sb("y_bias", [P, 2, hid])
        minus_half = sb("minus_half", [P, CH])

        x_in = sb("x_in", [P, CH, hid])
        y_buf = sb("y_buf", [P, 2, CH, hid])
        resid, y_tile = y_buf[:, 0], y_buf[:, 1]
        xn = sb("xn", [P, CH, hid])
        stats = sb("stats", [P, CH, 6])
        mean_var = sb("mean_var", [P, CH, 2])
        rstd = sb("rstd", [P, CH])
        xnT = sb("xnT", [P, 2, KT_, TOK], F32R)
        v_aug = sb("v_aug", [P, 2, CH, 2 * HALF * AUG])
        ffn_tok = sb("ffn_tok", [P, CH * leaves * 2 + CH * leaves // 2])
        gate = ffn_tok[:, 0:CH * leaves].rearrange("p (c n) -> p c n", c=CH)
        leaf_even = ffn_tok[:, CH * leaves:2 * CH * leaves].rearrange("p (c n) -> p c n", c=CH)
        leaf_odd = ffn_tok[:, 2 * CH * leaves:].rearrange("p (c n) -> p c n", c=CH)
        leafT = sb("leafT", [P, 2, LT, TOK], F32R)
        oT = sb("oT", [P, 2, PAIRS, TOK], F32R)

        kT = sb("kT", [P, 2, TOK])
        qT = sb("qT", [P, 2, TOK])
        ex = sb("ex", [P, 2, TOK])
        k_tok = sb("k_tok", [P, CH, P])
        aT = sb("aT", [P, 2, CH, P])
        state = sb("state", [P, PAIRS, 2 * AUG])
        snap = sb("snap", [P, CH - 1, 2 * AUG])
        o_tok = sb("o_tok", [P, CH, P])
        den = sb("den", [P, 4])
        rden = sb("rden", [P, 4])
        stage0 = sb("stage0", [P, KT_ * inner])

        stage_of = {"wv": stage0[:, :], "wk": y_buf[:, :, :, :].rearrange("p a c d -> p (a c d)"),
                    "wq": v_aug[:, 1].rearrange("p c n -> p (c n)")[:, 0:KT_ * inner], "wo": stage0[:, :]}
        small = [ffn_tok[:, i * 2 * hid:(i + 1) * 2 * hid].rearrange("p (t n) -> p t n", t=2) for i in range(4)]
        routers_in, tree_wq_in, leaf_in, wout_in = small
        routersT = aT[:, 0].rearrange("p c n -> p (c n)").rearrange("p (t n) -> p t n", t=2)
        leafvT = aT[:, 1].rearrange("p c n -> p (c n)").rearrange("p (t n) -> p t n", t=2)
        woutT = k_tok[:, :, :].rearrange("p c n -> p (c n)").rearrange("p (t n) -> p t n", t=2)

        def bank(name):
            return ctx.enter_context(nc.psum_tensor(name, [P, 512], F32))

        work = [bank("work0"), bank("work1")]
        s_bank = [bank("s_head0"), bank("s_head1")]
        o_bank = [bank("o_first"), bank("o_second")]
        kv_bank = bank("kv_bank")
        tr_bank = bank("tr_bank")

        def w(name):
            return work[bank_of(name)]

        loaded = {n: sem(f"{n}_loaded") for n in ("wv", "wk", "wq", "wo", "small", "bias", "bcast")}
        x_loaded = sem("x_loaded")
        x_consumed = sem("x_consumed")
        ident_ready = sem("ident_ready")
        consts_ready = sem("consts_ready")
        ones_ready = sem("ones_ready")
        split_hi = sem("split_hi")
        split_done = sem("split_done")
        biasT_filled = sem("biasT_filled")
        bias_ready = sem("bias_ready")
        treeT_filled = sem("treeT_filled")
        treeT_ready = sem("treeT_ready")
        route_filled = sem("route_filled")
        route_hi = sem("route_hi")
        route_ready = sem("route_ready")
        pool_step = sem("pool_step")
        stats_step = sem("stats_step")
        moments_ready = sem("moments_ready")
        rstd_ready = sem("rstd_ready")
        xn_ready = sem("xn_ready")
        work_filled = [sem("work0_filled"), sem("work1_filled")]
        work_drained = [sem("work0_drained"), sem("work1_drained")]
        hi_ready = sem("hi_ready")
        relu_ready = sem("relu_ready")
        exp_ready = sem("exp_ready")
        k_tr_filled = sem("k_tr_filled")
        k_tok_ready = sem("k_tok_ready")
        s_filled = sem("s_filled")
        s_copied = sem("s_copied")
        a_masked = sem("a_masked")
        kv_filled = sem("kv_filled")
        snap_step = sem("snap_step")
        snap_ready = sem("snap_ready")
        state_ready = sem("state_ready")
        state_reset = sem("state_reset")
        o_filled = sem("o_filled")
        den_step = sem("den_step")
        o_normed = sem("o_normed")
        o_tr_filled = sem("o_tr_filled")
        oT_hi = sem("oT_hi")
        oT_ready = sem("oT_ready")
        leaf_step = sem("leaf_step")
        leaf_ready = sem("leaf_ready")
        y_stored = sem("y_stored")

        def wait_apart(eng, semaphore, value):
            if isinstance(value, int):
                eng.wait_ge(semaphore, value)
                return
            eng.reg_mov(scratch[eng.engine], value)
            eng.wait_ge(ident_ready, 1)
            eng.wait_ge(semaphore, scratch[eng.engine])

        def passes(lhs, rhs):
            return ((lhs(0), rhs(0)), (lhs(0), rhs(1)), (lhs(1), rhs(0)))

        scratch = {eng.engine: eng.alloc_register("scratch") for eng in (nc.gpsimd, nc.vector, nc.tensor)}
        for eng in (nc.gpsimd, nc.vector, nc.tensor):
            eng.reg_mov(scratch[eng.engine], 0)

        block = ctx.enter_context(nc.Block())

        @block.sync
        def _(sp):
            sp.sem_inc(y_stored, AHEAD)
            sp.dma_start(x_in[:, :, :], x_rows[0]).then_inc(x_loaded, 16)
            for i, b in enumerate((bq, bk)):
                sp.dma_start(bias_rows[i * PAIRS:(i + 1) * PAIRS, :],
                             b.rearrange("(r n) -> r n", n=P)).then_inc(loaded["bias"], 16)
            for name, src in (("wv", Wv), ("wk", Wk), ("wq", Wq)):
                sp.dma_start(stage_of[name].rearrange("p (t n) -> p t n", t=KT_),
                             src.rearrange("(t p) n -> p t n", p=P)).then_inc(loaded[name], 16)
            sp.dma_start(bv_all[:, :], bv.partition_broadcast(P)).then_inc(loaded["bcast"], 16)
            sp.dma_start(y_bias[:, 0], bo.partition_broadcast(P)).then_inc(loaded["bcast"], 16)
            sp.dma_start(y_bias[:, 1], Wout_b.partition_broadcast(P)).then_inc(loaded["bcast"], 16)
            sp.wait_ge(consts_ready, 1)
            sp.dma_start(routers_in[:, 0], routers[0:P, :]).then_inc(loaded["small"], 16)
            sp.dma_start(routers_in[0:nodes - P, 1], routers[P:nodes, :]).then_inc(loaded["small"], 16)
            for dst, src in ((tree_wq_in, tree_Wq), (leaf_in, leaf_values), (wout_in, Wout_w)):
                sp.dma_start(dst, src.rearrange("(t p) n -> p t n", p=P)).then_inc(loaded["small"], 16)
            sp.wait_ge(split_done, 1)
            sp.dma_start(stage_of["wo"].rearrange("p (t n) -> p t n", t=PAIRS),
                         Wo.rearrange("(t p) n -> p t n", p=P)).then_inc(loaded["wo"], 16)

            def store(g):
                for i in range(2):
                    sp.wait_ge(work_drained[bank_of(f"y{i}")], count_of(f"y{i}", g))
                    sp.dma_start(out_rows[bass.ds(g, 1), :, 2 * i:2 * i + 2, :].rearrange("a p c d -> (a p) c d"),
                                 y_tile[:, 2 * i:2 * i + 2, :]).then_inc(y_stored, 16)

            last = batches * MACROS - 1
            with sp.Fori(0, last) as g:
                sp.wait_ge(x_consumed, g + 1)
                sp.dma_start(x_in[:, :, :], x_rows[bass.ds(g + 1, 1)].rearrange("a p c d -> (a p) c d"))\
                  .then_inc(x_loaded, 16)
                store(g)
            sp.wait_ge(x_consumed, last + 1)
            sp.dma_start(x_in[:, :, :], x_rows[0]).then_inc(x_loaded, 16)
            store(last)
            sp.wait_ge(y_stored, AHEAD + 32 * (last + 1))
            sp.wait_ge(x_loaded, 16 * (last + 2))

        @block.gpsimd
        def _(pool):
            pool.memset(routers_in[:, 1], 0.0).then_inc(consts_ready, 1)
            pool.memset(ident[:, :], 0.0).then_inc(pool_step, 1)
            pool.wait_ge(pool_step, 1)
            pool.affine_select(out=ident[:, :], in_=ident[:, :], compare_op=ALU.not_equal, fill=1.0, base=0,
                               pattern=[[-1, P]], channel_multiplier=1).then_inc(ident_ready, 1)
            pool.memset(minus_half[:, :], -0.5).then_inc(pool_step, 1)

            def ones(half):
                heads = v_aug[:, half].rearrange("p c (h e) -> p c h e", e=AUG)
                pool.memset(heads[:, :, :, D:AUG].rearrange("p c h e -> p c (h e)"), 1.0)\
                    .then_inc(ones_ready, 1)

            def inverse_deviation(count):
                wait_apart(pool, moments_ready, count)
                pool.tensor_scalar(rstd[:, :], mean_var[:, :, 1], EPS_NORM, None, ALU.add).then_inc(rstd_ready, 1)
                pool.wait_ge(rstd_ready, 2 * count - 1)
                pool.tensor_tensor(rstd[:, :], rstd[:, :], minus_half[:, :], ALU.pow).then_inc(rstd_ready, 1)

            pool.wait_ge(pool_step, 2)
            inverse_deviation(1)
            ones(0)
            pool.wait_ge(split_done, 3)
            ones(1)
            pool.wait_ge(treeT_ready, 3)
            pool.wait_ge(loaded["bcast"], 48)
            pool.tensor_tensor(y_bias[:, 0], y_bias[:, 0], y_bias[:, 1], ALU.add).then_inc(pool_step, 1)
            pool.wait_ge(pool_step, 3)

            LEVEL_STEPS = 2 * depth + 1

            def level(l, g):
                n = 1 << l
                bufs = (leaf_even, leaf_odd)
                src, dst = bufs[l % 2], bufs[(l + 1) % 2]
                kids = dst[:, :, 0:2 * n].rearrange("p c (n k) -> p c n k", k=2)
                left, right = kids[:, :, :, 0], kids[:, :, :, 1]
                g_l = gate[:, :, n - 1:2 * n - 1]
                wait_apart(pool, leaf_step, g * LEVEL_STEPS + 2 * l + 1)
                if l == 0:
                    pool.tensor_copy(right, g_l).then_inc(leaf_step, 1)
                    pool.tensor_scalar(left, g_l, -1.0, 1.0, ALU.mult, ALU.add).then_inc(leaf_step, 1)
                    return
                pool.tensor_tensor(right, src[:, :, 0:n], g_l, ALU.mult).then_inc(leaf_step, 1)
                pool.wait_ge(leaf_step, g * LEVEL_STEPS + 2 * l + 2)
                last = pool.tensor_tensor(left, src[:, :, 0:n], right, ALU.subtract)
                last.then_inc(leaf_step, 1)

            def unit(p, g):
                for h in range(2):
                    wait_apart(pool, s_copied, g * (2 * PAIRS) + (AHEAD + 2 * p + h + 1))
                    pool.affine_select(out=aT[:, h], in_=aT[:, h], compare_op=ALU.is_ge, fill=0.0, base=0,
                                       pattern=[[0, CH], [1, P]], channel_multiplier=-1).then_inc(a_masked, 1)
                if p == 0:
                    pool.wait_ge(work_drained[bank_of("y1")], count_before("y1", g))
                    pool.wait_ge(x_loaded, g * 16 + 16)
                    pool.tensor_tensor(resid, x_in[:, :, :],
                                       y_bias[:, 0].unsqueeze(1).to_broadcast([P, CH, hid]), ALU.add)\
                        .then_inc(x_consumed, 1)
                    for i in range(2):
                        wait_apart(pool, work_drained[bank_of(f"gate{i}")], count_before(f"gate{i}", g))
                    pool.tensor_scalar(gate, gate, 0.5, 0.5, ALU.mult, ALU.add).then_inc(leaf_step, 1)
                if p < CH:
                    for l in range(p * depth // CH, (p + 1) * depth // CH):
                        level(l, g)
                if p == PAIRS - 2:
                    inverse_deviation(g + 2)

            with pool.Fori(0, batches) as b:
                with pool.Fori(0, MACROS) as m:
                    g = pool.snap(b * MACROS + m)
                    for p in range(PAIRS):
                        unit(p, g)

        @block.scalar
        def _(act):
            def split(name, dst, count):
                act.wait_ge(loaded[name], 16)
                act.activation(dst[:, 0].rearrange("p t n -> p (t n)"), stage_of[name], ACT.Copy)\
                   .then_inc(split_hi, 1)

            def hi_of_work(name, count, dst, n_cols=TOK):
                act.wait_ge(work_filled[bank_of(name)], count)
                act.activation(dst, w(name)[:, 0:n_cols], ACT.Copy).then_inc(hi_ready, 1)

            def exponential(name, count, done):
                kind, p = name[0], int(name[1:])
                slot = 0 if kind == "K" else 1
                col = p + (PAIRS if kind == "K" else 0)
                act.wait_ge(work_filled[bank_of(name)], count)
                act.activation(ex[:, slot], w(name)[:, :], ACT.Relu, scale=-1.0, bias=neg_bias[:, col:col + 1])\
                   .then_inc(relu_ready, 1)
                act.wait_ge(relu_ready, done + 1)
                act.activation(ex[:, slot], ex[:, slot], ACT.Exp, scale=-1.0).then_inc(exp_ready, 1)

            def half_gates(i, count):
                act.wait_ge(work_filled[bank_of(f"gate{i}")], count)
                act.activation(gate[:, 2 * i:2 * i + 2, :].rearrange("p c n -> p (c n)"), w(f"gate{i}")[:, :],
                               ACT.Tanh, scale=0.5).then_inc(work_drained[bank_of(f"gate{i}")], 1)

            def copy_oT(p, g):
                act.wait_ge(o_tr_filled, g * PAIRS + (p + 1))
                act.activation(oT[:, 0, p], tr_bank[:, :], ACT.Copy).then_inc(oT_hi, 1)

            act.sem_inc(s_copied, AHEAD)
            split("wv", wv, 1)
            for t in range(KT_):
                hi_of_work(f"xnT{t}", first_count(f"xnT{t}"), xnT[:, 0, t])
            split("wk", wk, 2)
            split("wq", wq, 3)
            act.wait_ge(bias_ready, 2)
            for i, name in enumerate(("K0", "Q0")):
                exponential(name, first_count(name), i)
            for i, (src, dst) in enumerate(((s_bank[0], routersT), (s_bank[1], leafvT), (o_bank[0], woutT))):
                act.wait_ge(treeT_filled, i + 1)
                act.activation(dst.rearrange("p t n -> p (t n)"), src[:, :], ACT.Copy).then_inc(treeT_ready, 1)
            act.wait_ge(route_filled, 1)
            act.activation(route[:, 0].rearrange("p t n -> p (t n)"), kv_bank[:, :], ACT.Copy).then_inc(route_hi, 1)
            for i in range(2):
                half_gates(i, first_count(f"gate{i}"))
            for i in range(LT):
                act.wait_ge(work_filled[i], first_count(f"tree_out{i}"))
                act.activation(tree_w[:, 0, i], work[i][:, 0:hid], ACT.Copy).then_inc(hi_ready, 1)
            split("wo", wo, 4)

            PHI = 2 * PAIRS

            def unit(p, g):
                act.wait_ge(k_tr_filled, g * PAIRS + (p + 1))
                act.activation(k_tok[:, :, :].rearrange("p c n -> p (c n)"), tr_bank[:, :], ACT.Copy)\
                   .then_inc(k_tok_ready, 1)
                if p < PAIRS - 1:
                    exponential(f"K{p + 1}", count_of(f"K{p + 1}", g), g * PHI + (2 + 2 * p))
                else:
                    hi_of_work("xnT0", count_of("xnT0", g), xnT[:, 0, 0])
                if p > 0:
                    copy_oT(p - 1, g)
                for h in range(2):
                    act.wait_ge(s_filled, g * (2 * PAIRS) + (2 * p + h + 1))
                    act.activation(aT[:, h].rearrange("p c n -> p (c n)"), s_bank[h][:, :], ACT.Copy)\
                       .then_inc(s_copied, 1)
                if p < PAIRS - 1:
                    exponential(f"Q{p + 1}", count_of(f"Q{p + 1}", g), g * PHI + (3 + 2 * p))
                else:
                    hi_of_work("xnT1", count_of("xnT1", g), xnT[:, 0, 1])
                if CH <= p < CH + LT:
                    t = p - CH
                    hi_of_work(f"leafT{t}", count_of(f"leafT{t}", g), leafT[:, 0, t])

            with act.Fori(0, batches) as b:
                with act.Fori(0, MACROS) as m:
                    g = act.snap(b * MACROS + m)
                    for p in range(PAIRS):
                        unit(p, g)
                    copy_oT(PAIRS - 1, g)
                    for i, name in enumerate(("K0", "Q0")):
                        exponential(name, count_of(name, g), g * PHI + (2 + 2 * (PAIRS - 1) + i))
                    for i in range(2):
                        half_gates(i, count_of(f"gate{i}", g))

        @block.vector
        def _(dve):
            def layer_norm(count):
                dve.wait_ge(x_loaded, count * 16)
                for c in range(CH):
                    dve.bn_stats(stats[:, c], x_in[:, c]).then_inc(stats_step, 1)
                for c in range(CH):
                    wait_apart(dve, stats_step, count * CH + (c + 1 - CH))
                    last = dve.bn_aggr(mean_var[:, c], stats[:, c])
                last.then_inc(moments_ready, 1)

            def normalise(count):
                dve.wait_ge(moments_ready, count)
                dve.wait_ge(rstd_ready, 2 * count)
                for c in range(CH):
                    last = dve.tensor_scalar(xn[:, c], x_in[:, c], mean_var[:, c, 0:1], rstd[:, c:c + 1],
                                             ALU.subtract, ALU.mult)
                last.then_inc(xn_ready, 1)

            def split(name, dst, count):
                dve.wait_ge(split_hi, count)
                dve.tensor_tensor(dst[:, 1].rearrange("p t n -> p (t n)"), stage_of[name],
                                  dst[:, 0].bitcast(F32).rearrange("p t n -> p (t n)"), ALU.subtract)\
                   .then_inc(split_done, 1)

            def lo_of_work(name, dst, hi, done):
                dve.wait_ge(hi_ready, done)
                dve.tensor_tensor(dst, w(name)[:, :], hi.bitcast(F32), ALU.subtract)\
                   .then_inc(work_drained[bank_of(name)], 1)

            def phi(name, done):
                kind, p = name[0], int(name[1:])
                slot, dst = (0, kT) if kind == "K" else (1, qT)
                col = p + (PAIRS if kind == "K" else 0)
                dve.wait_ge(exp_ready, done)
                dve.scalar_tensor_tensor(out=dst[:, p % 2], in0=w(name)[:, :], scalar=bias_one[:, col:col + 1],
                                         in1=ex[:, slot], op0=ALU.add, op1=ALU.max)\
                   .then_inc(work_drained[bank_of(name)], 1)

            def values(name, count):
                half, c = int(name[1]), int(name[3:])
                n = 2 * HALF * D
                dst = v_aug[:, half, c].rearrange("p (h e) -> p h e", e=AUG)[:, :, 0:D]
                dve.wait_ge(work_filled[bank_of(name)], count)
                dve.tensor_tensor(dst, w(name)[:, :].rearrange("p (h e) -> p h e", e=D),
                                  bv_all[:, half * n:(half + 1) * n].rearrange("p (h e) -> p h e", e=D), ALU.add)\
                   .then_inc(work_drained[bank_of(name)], 1)

            for counter in (state_ready, o_normed, oT_ready):
                dve.sem_inc(counter, AHEAD)
            layer_norm(1)
            normalise(1)
            split("wv", wv, 1)
            dve.wait_ge(biasT_filled, 1)
            dve.tensor_scalar(neg_bias[:, :], tr_bank[:, 0:2 * PAIRS], -1.0, None, ALU.mult).then_inc(bias_ready, 1)
            dve.tensor_scalar(bias_one[:, :], tr_bank[:, 0:2 * PAIRS], 1.0, None, ALU.add).then_inc(bias_ready, 1)
            for t in range(KT_):
                lo_of_work(f"xnT{t}", xnT[:, 1, t], xnT[:, 0, t], t + 1)
            split("wk", wk, 2)
            dve.wait_ge(loaded["bcast"], 48)
            for c in range(2):
                values(f"V0c{c}", first_count(f"V0c{c}"))
            split("wq", wq, 3)
            for c in range(2, CH):
                values(f"V0c{c}", first_count(f"V0c{c}"))
            for i, name in enumerate(("K0", "Q0")):
                phi(name, i + 1)
            dve.wait_ge(route_hi, 1)
            dve.tensor_tensor(route[:, 1].rearrange("p t n -> p (t n)"), kv_bank[:, :],
                              route[:, 0].bitcast(F32).rearrange("p t n -> p (t n)"), ALU.subtract)\
               .then_inc(route_ready, 1)
            for i in range(LT):
                dve.wait_ge(hi_ready, KT_ + i + 1)
                dve.tensor_tensor(tree_w[:, 1, i], work[i][:, 0:hid], tree_w[:, 0, i].bitcast(F32), ALU.subtract)\
                   .then_inc(work_drained[i], 1)
            split("wo", wo, 4)
            dve.wait_ge(ones_ready, 2)

            HI_FIRST = KT_ + LT
            HI = KT_ + LT

            def add_state(c, before, after, step, sem_, inc):
                off = (c % 2) * 2 * AUG
                for h in range(2):
                    rows, cols = slice(h * D, (h + 1) * D), slice(h * AUG, (h + 1) * AUG)
                    last = dve.tensor_tensor(after[rows, cols], kv_bank[rows, off + h * AUG:off + (h + 1) * AUG],
                                             before[rows, cols], ALU.add)
                last.then_inc(sem_, inc)

            def norm(i, p, g):
                v = o_bank[i][:, 0:4 * AUG].rearrange("p (n e) -> p n e", e=AUG)
                n = 2 * p + i
                dve.wait_ge(o_filled, g * (2 * PAIRS) + (n + 1))
                dve.tensor_scalar(den[:, :], v[:, :, D], EPS_ATTN, None, ALU.add).then_inc(den_step, 1)
                dve.wait_ge(den_step, g * (4 * PAIRS) + (2 * n + 1))
                dve.reciprocal(rden[:, :], den[:, :]).then_inc(den_step, 1)
                dve.wait_ge(den_step, g * (4 * PAIRS) + (2 * n + 2))
                dst = o_tok[:, 2 * i:2 * i + 2].rearrange("p c (h e) -> p (c h) e", e=D)
                dve.tensor_tensor(dst, v[:, :, 0:D], rden[:, :].unsqueeze(2).to_broadcast([P, 4, D]), ALU.mult)\
                   .then_inc(o_normed, 1)

            def lo_of_oT(p, g):
                dve.wait_ge(oT_hi, g * PAIRS + (p + 1))
                dve.tensor_tensor(oT[:, 1, p], tr_bank[:, :], oT[:, 0, p].bitcast(F32), ALU.subtract)\
                   .then_inc(oT_ready, 1)

            PHI = 2 * PAIRS

            def unit(p, g):
                if p < PAIRS - 1:
                    phi(f"K{p + 1}", g * PHI + (2 + 2 * p + 1))
                else:
                    lo_of_work("xnT0", xnT[:, 1, 0], xnT[:, 0, 0], g * HI + (HI_FIRST + LT + 1))
                if p > 0:
                    lo_of_oT(p - 1, g)
                dve.wait_ge(kv_filled, g * (2 * PAIRS) + (2 * p + 1))
                add_state(0, state[:, p], snap[:, 0], 0, snap_step, 1)
                dve.wait_ge(snap_step, g * PAIRS + (p + 1))
                add_state(1, snap[:, 0], snap[:, 1], 1, snap_ready, 1)
                if p < PAIRS - 1:
                    phi(f"Q{p + 1}", g * PHI + (2 + 2 * p + 2))
                else:
                    lo_of_work("xnT1", xnT[:, 1, 1], xnT[:, 0, 1], g * HI + (HI_FIRST + LT + 2))
                dve.wait_ge(kv_filled, g * (2 * PAIRS) + (2 * p + 2))
                dve.wait_ge(snap_ready, g * (2 * PAIRS) + (2 * p + 1))
                add_state(2, snap[:, 1], snap[:, 2], 2, snap_ready, 1)
                norm(0, p, g)
                dve.wait_ge(snap_ready, g * (2 * PAIRS) + (2 * p + 2))
                add_state(3, snap[:, 2], state[:, p], 3, state_ready, 1)
                if p < CH:
                    values(f"V1c{p}", count_of(f"V1c{p}", g))
                elif p < CH + LT:
                    t = p - CH
                    lo_of_work(f"leafT{t}", leafT[:, 1, t], leafT[:, 0, t], g * HI + (HI_FIRST + t + 1))
                norm(1, p, g)
                if p == PAIRS - 3:
                    layer_norm(g + 2)
                if p == PAIRS - 2:
                    normalise(g + 2)

            with dve.Fori(0, batches) as b:
                dve.wait_ge(state_ready, b * (MACROS * PAIRS) + AHEAD)
                dve.memset(state[:, :, :], 0.0).then_inc(state_reset, 1)
                dve.wait_ge(state_reset, b * 2 + 1)
                dve.memset(snap[:, :, :], 0.0).then_inc(state_reset, 1)
                wait_apart(dve, state_reset, b * 2 + 2)
                with dve.Fori(0, MACROS) as m:
                    g = dve.snap(b * MACROS + m)
                    for p in range(PAIRS):
                        unit(p, g)
                    for c in range(2):
                        values(f"V0c{c}", count_of(f"V0c{c}", g))
                    lo_of_oT(PAIRS - 1, g)
                    for c in range(2, CH):
                        values(f"V0c{c}", count_of(f"V0c{c}", g))
                    for i, name in enumerate(("K0", "Q0")):
                        phi(name, g * PHI + (2 + 2 * (PAIRS - 1) + i + 1))
                    dve.wait_ge(y_stored, g * 32 + AHEAD)
                    for i in range(2):
                        name = f"y{i}"
                        dve.wait_ge(work_filled[bank_of(name)], count_of(name, g))
                        dve.tensor_tensor(y_tile[:, 2 * i:2 * i + 2], w(name)[:, :].rearrange("p (c d) -> p c d", d=hid),
                                          resid[:, 2 * i:2 * i + 2], ALU.add)\
                           .then_inc(work_drained[bank_of(name)], 1)

        @block.tensor
        def _(pe):
            def split_product(dst, lhs, rhs, tiles):
                steps = [s for t in range(tiles) for s in passes(lambda a, t=t: lhs(a, t), lambda a, t=t: rhs(a, t))]
                for i, (l, r) in enumerate(steps):
                    last = pe.matmul(dst, l, r, start=i == 0, stop=i == len(steps) - 1)
                return last

            def fill(name):
                dst = w(name) if name in FILLS else work[FIRST_FILLS.index(name) % 2]
                if name[0] in "KQ":
                    wt, p = (wk if name[0] == "K" else wq), int(name[1:])
                    return split_product(dst[:, :], lambda a, t: wt[:, a, t, p * P:(p + 1) * P],
                                         lambda a, t: xnT[:, a, t], KT_)
                if name[0] == "V":
                    half, c, n = int(name[1]), int(name[3:]), 2 * HALF * D
                    return split_product(dst[:, 0:n], lambda a, t: xnT[:, a, t, c * P:(c + 1) * P],
                                         lambda a, t: wv[:, a, t, half * n:(half + 1) * n], KT_)
                if name.startswith("xnT") or name.startswith("leafT"):
                    t, src = int(name[-1]), xn if name[0] == "x" else leaf_even
                    for c in range(CH):
                        last = pe.transpose(dst[:, c * P:(c + 1) * P], src[:, c, t * P:(t + 1) * P], ident[:, :])
                    return last
                if name.startswith("gate"):
                    i = int(name[-1])
                    for j in range(2):
                        c = 2 * i + j
                        last = split_product(dst[:, j * leaves:(j + 1) * leaves],
                                             lambda a, t: xnT[:, a, t, c * P:(c + 1) * P],
                                             lambda a, t: route[:, a, t], KT_)
                    return last
                if name.startswith("tree_out"):
                    i = int(name[-1])
                    for t in range(KT_):
                        last = pe.matmul(dst[:, 0:hid], leafvT[:, t, i * P:(i + 1) * P], woutT[:, t],
                                         start=t == 0, stop=t == KT_ - 1)
                    return last
                i = int(name[-1])
                for j in range(2):
                    c = 2 * i + j
                    cols = slice(c * P, (c + 1) * P)
                    last = split_product(dst[:, j * hid:(j + 1) * hid],
                                         lambda a, t: oT[:, a, t, cols] if t < PAIRS else leafT[:, a, t - PAIRS, cols],
                                         lambda a, t: wo[:, a, t] if t < PAIRS else tree_w[:, a, t - PAIRS],
                                         PAIRS + LT)
                return last

            def first_fill(name):
                i = FIRST_FILLS.index(name)
                if i >= 2:
                    pe.wait_ge(work_drained[i % 2], i // 2)
                fill(name).then_inc(work_filled[i % 2], 1)

            def loop_fill(name, g):
                pe.wait_ge(work_drained[bank_of(name)], g * PER_BANK + (FIRST_PER_BANK + FILLS.index(name) // 2))
                fill(name).then_inc(work_filled[bank_of(name)], 1)

            pe.wait_ge(ident_ready, 1)
            pe.wait_ge(loaded["bias"], 32)
            pe.transpose(tr_bank[:, 0:2 * PAIRS], bias_rows[:, :], ident[0:2 * PAIRS, 0:2 * PAIRS])\
              .then_inc(biasT_filled, 1)
            pe.wait_ge(xn_ready, 1)
            first_fill("xnT0")
            first_fill("xnT1")
            pe.wait_ge(split_done, 1)
            for c in range(CH):
                if c == 0:
                    pe.wait_ge(work_drained[1], 1)
                first_fill(f"V0c{c}")
            pe.wait_ge(split_done, 2)
            first_fill("K0")
            pe.wait_ge(split_done, 3)
            first_fill("Q0")
            pe.wait_ge(loaded["small"], 80)
            for src, dst in ((routers_in, s_bank[0]), (leaf_in, s_bank[1]), (wout_in, o_bank[0])):
                v = dst[:, :].rearrange("p (t n) -> p t n", t=2)
                for i in range(2):
                    for j in range(2):
                        last = pe.transpose(v[:, i, j * P:(j + 1) * P], src[:, j, i * P:(i + 1) * P], ident[:, :])
                last.then_inc(treeT_filled, 1)
            pe.wait_ge(treeT_ready, 3)
            for i in range(KT_):
                for t in range(KT_):
                    last = pe.matmul(kv_bank[:, i * leaves:(i + 1) * leaves], tree_wq_in[:, t, i * P:(i + 1) * P],
                                     routersT[:, t], start=t == 0, stop=t == KT_ - 1)
            last.then_inc(route_filled, 1)
            pe.wait_ge(route_ready, 1)
            first_fill("gate0")
            first_fill("gate1")
            first_fill("tree_out0")
            first_fill("tree_out1")
            pe.wait_ge(split_done, 4)

            def transpose_o(p, g):
                pe.wait_ge(o_normed, g * (2 * PAIRS) + (AHEAD + 2 * p + 2))
                pe.wait_ge(k_tok_ready, g * PAIRS + min(p + 2, PAIRS))
                for c in range(CH):
                    last = pe.transpose(tr_bank[:, c * P:(c + 1) * P], o_tok[:, c], ident[:, :])
                last.then_inc(o_tr_filled, 1)

            def outer_products(i, p, g):
                half, off = p // HALF, (p % HALF) * 2 * AUG
                for c in (2 * i, 2 * i + 1):
                    last = pe.matmul(kv_bank[:, (c % 2) * 2 * AUG:(c % 2 + 1) * 2 * AUG], k_tok[:, c],
                                     v_aug[:, half, c, off:off + 2 * AUG], start=True, stop=True)
                last.then_inc(kv_filled, 1)

            def attend(i, p, g):
                half = p // HALF
                for c in (2 * i, 2 * i + 1):
                    at = (c % 2) * 2 * AUG
                    before = state[:, p] if c == 0 else snap[:, c - 1]
                    pe.matmul(o_bank[i][:, at:at + 2 * AUG], qT[:, p % 2, c * P:(c + 1) * P], before,
                              start=True, stop=False)
                    for h in range(2):
                        off = (2 * (p % HALF) + h) * AUG
                        last = pe.matmul(o_bank[i][:, at + h * AUG:at + (h + 1) * AUG], aT[:, h, c],
                                         v_aug[:, half, c, off:off + AUG], start=False, stop=h == 1)
                last.then_inc(o_filled, 1)

            def unit(p, g):
                if p == 0:
                    pe.wait_ge(work_drained[bank_of("K0")], count_before("K0", g))
                    pe.wait_ge(oT_ready, g * PAIRS + AHEAD)
                elif p == 1:
                    pe.wait_ge(work_drained[bank_of("K1")], count_of("K1", g))
                    pe.wait_ge(k_tok_ready, g * PAIRS + 1)
                else:
                    pe.wait_ge(work_drained[bank_of(f"K{p}")], count_of(f"K{p}", g))
                    pe.wait_ge(oT_ready, g * PAIRS + (AHEAD + p - 1))
                for c in range(CH):
                    last = pe.transpose(tr_bank[:, c * P:(c + 1) * P], kT[:, p % 2, c * P:(c + 1) * P], ident[:, :])
                last.then_inc(k_tr_filled, 1)
                if p < PAIRS - 1:
                    loop_fill(f"K{p + 1}", g)
                else:
                    pe.wait_ge(xn_ready, g + 2)
                    loop_fill("xnT0", g)
                if p > 0:
                    transpose_o(p - 1, g)
                if p == 0:
                    pe.wait_ge(work_drained[bank_of("Q0")], count_before("Q0", g))
                else:
                    pe.wait_ge(work_drained[bank_of(f"Q{p}")], count_of(f"Q{p}", g))
                pe.wait_ge(s_copied, g * (2 * PAIRS) + (AHEAD + 2 * p))
                for c in range(CH):
                    for h in range(2):
                        rows, cols = slice(h * D, (h + 1) * D), slice(c * P, (c + 1) * P)
                        last = pe.matmul(s_bank[h][:, cols], kT[rows, p % 2, cols], qT[rows, p % 2, cols],
                                         start=True, stop=True)
                        if c == CH - 1:
                            last.then_inc(s_filled, 1)
                if p == HALF:
                    pe.wait_ge(work_drained[bank_of("V1c3")], count_of("V1c3", g))
                    pe.wait_ge(work_drained[bank_of("V1c2")], count_of("V1c2", g))
                pe.wait_ge(k_tok_ready, g * PAIRS + (p + 1))
                pe.wait_ge(state_ready, g * PAIRS + (AHEAD + p))
                outer_products(0, p, g)
                if p < PAIRS - 1:
                    loop_fill(f"Q{p + 1}", g)
                else:
                    loop_fill("xnT1", g)
                pe.wait_ge(snap_ready, g * (2 * PAIRS) + (2 * p + 1))
                outer_products(1, p, g)
                pe.wait_ge(a_masked, g * (2 * PAIRS) + (2 * p + 2))
                pe.wait_ge(o_normed, g * (2 * PAIRS) + (AHEAD + 2 * p))
                attend(0, p, g)
                if p < CH:
                    loop_fill(f"V1c{p}", g)
                elif p < CH + LT:
                    if p == CH:
                        pe.wait_ge(leaf_step, (g + 1) * (2 * depth + 1))
                    loop_fill(f"leafT{p - CH}", g)
                pe.wait_ge(snap_ready, g * (2 * PAIRS) + (2 * p + 2))
                attend(1, p, g)

            with pe.Fori(0, batches) as b:
                wait_apart(pe, state_reset, b * 2 + 2)
                with pe.Fori(0, MACROS) as m:
                    g = pe.snap(b * MACROS + m)
                    for p in range(PAIRS):
                        unit(p, g)
                    for t in range(KT_):
                        pe.wait_ge(work_drained[bank_of(f"xnT{t}")], count_of(f"xnT{t}", g))
                    for c in range(2):
                        loop_fill(f"V0c{c}", g)
                    transpose_o(PAIRS - 1, g)
                    for name in ("V0c2", "V0c3", "K0", "Q0", "gate0", "gate1"):
                        loop_fill(name, g)
                    pe.wait_ge(oT_ready, g * PAIRS + (AHEAD + PAIRS))
                    loop_fill("y0", g)
                    loop_fill("y1", g)


_INS = ['L0_attn_x', 'L0_attn_Wq', 'L0_attn_bq', 'L0_attn_Wk', 'L0_attn_bk', 'L0_attn_Wv', 'L0_attn_bv',
        'L0_attn_Wo', 'L0_attn_bo', 'L0_ffn_Wq', 'L0_ffn_routers', 'L0_ffn_leaf_keys', 'L0_ffn_leaf_values',
        'L0_ffn_Wout_w', 'L0_ffn_Wout_b']


def kernel(**inputs):
    import numpy as _np
    import concourse.bacc as _bacc
    from concourse import mybir as _mybir
    from concourse.bass_utils import run_bass_kernel_spmd as _run

    nc = _bacc.Bacc("TRN2", target_bir_lowering=False, num_devices=1)
    arrays, args = {}, []
    for name in _INS:
        a = _np.ascontiguousarray(inputs[name])
        arrays[f"in_{name}_dram"] = a
        args.append(nc.dram_tensor(f"in_{name}_dram", a.shape, _mybir.dt.from_np(a.dtype), kind="ExternalInput").ap())
    shape = inputs['L0_attn_x'].shape
    out = nc.dram_tensor("out_dram", shape, _mybir.dt.float32, kind="ExternalOutput").ap()
    attention_and_tree_layer(nc, *args, out)
    r = _run(nc, [arrays], core_ids=[0])
    return r.results[0]["out_dram"]
```

```python
from contextlib import ExitStack

import concourse.bass as bass
from concourse import mybir

ALU = mybir.AluOpType
ACT = mybir.ActivationFunctionType
F32 = mybir.dt.float32
F32R = mybir.dt.float32r

P = 128
HEADS, D = 16, 64
PAIRS = HEADS // 2
TOK = 512
CH = TOK // P
AUG = D + 1
HALF = PAIRS // 2
EPS_ATTN = 1e-6
EPS_NORM = 1e-5
AHEAD = 1

FIRST_FILLS = (["xnT0", "xnT1"] + [f"V0c{c}" for c in range(CH)] + ["K0", "tree_out0", "Q0", "tree_out1",
                                                                  "gate0", "gate1"])
FILLS = []
for _p in range(PAIRS - 1):
    FILLS += [f"K{_p + 1}", f"Q{_p + 1}"]
    if _p < CH:
        FILLS.append(f"V1c{_p}")
    elif _p < CH + 2:
        FILLS.append(f"leafT{_p - CH}")
FILLS += ["xnT0", "xnT1"] + [f"V0c{c}" for c in range(CH)] + ["K0", "y0", "Q0", "y1", "gate0", "gate1"]
PER_BANK = len(FILLS) // 2
FIRST_PER_BANK = len(FIRST_FILLS) // 2
assert len(FILLS) % 2 == 0 and len(FIRST_FILLS) % 2 == 0


def bank_of(name):
    return FILLS.index(name) % 2


def count_of(name, g):
    return g * PER_BANK + (FIRST_PER_BANK + FILLS.index(name) // 2 + 1)


def count_before(name, g):
    return g * PER_BANK + (FIRST_PER_BANK + FILLS.index(name) // 2 + 1 - PER_BANK)


def first_count(name):
    return FIRST_FILLS.index(name) // 2 + 1


def attention_and_tree_layer(nc, x, Wq, bq, Wk, bk, Wv, bv, Wo, bo,
                             tree_Wq, routers, leaf_keys, leaf_values, Wout_w, Wout_b, out):
    batches, seq, hid = x.shape
    KT_ = hid // P
    MACROS = seq // TOK
    inner = HEADS * D
    leaves = leaf_values.shape[0]
    nodes = routers.shape[0]
    depth = leaves.bit_length() - 1
    LT = leaves // P
    assert KT_ == 2 and LT == 2 and nodes == leaves - 1 and Wq.shape[1] == inner

    x_rows = x.rearrange("b (t c p) d -> (b t) p c d", c=CH, p=P)
    out_rows = out.rearrange("b (t c p) d -> (b t) p c d", c=CH, p=P)

    with ExitStack() as ctx:
        def sb(name, shape, dt=F32):
            return ctx.enter_context(nc.sbuf_tensor(name, shape, dt))

        def sem(name):
            return ctx.enter_context(nc.semaphore(name))

        wq = sb("wq", [P, 2, KT_, inner], F32R)
        wk = sb("wk", [P, 2, KT_, inner], F32R)
        wv = sb("wv", [P, 2, KT_, inner], F32R)
        wo = sb("wo", [P, 2, PAIRS, hid], F32R)
        route = sb("route", [P, 2, KT_, leaves], F32R)
        tree_w = sb("tree_w", [P, 2, LT, hid], F32R)

        ident = sb("ident", [P, P])
        bias_rows = sb("bias_rows", [2 * PAIRS, P])
        neg_bias = sb("neg_bias", [P, 2 * PAIRS])
        bias_one = sb("bias_one", [P, 2 * PAIRS])
        bv_all = sb("bv_all", [P, inner])
        y_bias = sb("y_bias", [P, 2, hid])
        minus_half = sb("minus_half", [P, CH])

        x_in = sb("x_in", [P, CH, hid])
        y_buf = sb("y_buf", [P, 2, CH, hid])
        resid, y_tile = y_buf[:, 0], y_buf[:, 1]
        xn = sb("xn", [P, CH, hid])
        stats = sb("stats", [P, CH, 6])
        mean_var = sb("mean_var", [P, CH, 2])
        rstd = sb("rstd", [P, CH])
        xnT = sb("xnT", [P, 2, KT_, TOK], F32R)
        v_aug = sb("v_aug", [P, 2, CH, 2 * HALF * AUG])
        ffn_tok = sb("ffn_tok", [P, CH * leaves * 2 + CH * leaves // 2])
        gate = ffn_tok[:, 0:CH * leaves].rearrange("p (c n) -> p c n", c=CH)
        leaf_even = ffn_tok[:, CH * leaves:2 * CH * leaves].rearrange("p (c n) -> p c n", c=CH)
        leaf_odd = ffn_tok[:, 2 * CH * leaves:].rearrange("p (c n) -> p c n", c=CH)
        leafT = sb("leafT", [P, 2, LT, TOK], F32R)
        oT = sb("oT", [P, 2, PAIRS, TOK], F32R)

        kT = sb("kT", [P, 2, TOK])
        qT = sb("qT", [P, 2, TOK])
        ex = sb("ex", [P, 2, TOK])
        k_tok = sb("k_tok", [P, CH, P])
        k_split = sb("k_split", [P, 2, TOK], F32R)
        aT = sb("aT", [P, CH, 2, P])
        state = sb("state", [P, PAIRS, 2 * AUG])
        snap = sb("snap", [P, CH - 1, 2 * AUG])
        o_tok = sb("o_tok", [P, CH, P])
        den = sb("den", [P, 4])
        rden = sb("rden", [P, 4])
        with nc.sbuf_tensor("stage0", [P, KT_ * inner], F32) as stage0:
            pass
        q_split = sb("q_split", [P, 2, CH, 2, P], F32R)

        stage_of = {"wv": stage0[:, :], "wk": y_buf[:, :, :, :].rearrange("p a c d -> p (a c d)"),
                    "wq": v_aug[:, 1].rearrange("p c n -> p (c n)")[:, 0:KT_ * inner], "wo": stage0[:, :]}
        small = [ffn_tok[:, i * 2 * hid:(i + 1) * 2 * hid].rearrange("p (t n) -> p t n", t=2) for i in range(4)]
        routers_in, tree_wq_in, leaf_in, wout_in = small
        routersT = aT[:, 0:2].rearrange("p c h n -> p (c h n)").rearrange("p (t n) -> p t n", t=2)
        leafvT = aT[:, 2:4].rearrange("p c h n -> p (c h n)").rearrange("p (t n) -> p t n", t=2)
        woutT = k_tok[:, :, :].rearrange("p c n -> p (c n)").rearrange("p (t n) -> p t n", t=2)

        def bank(name):
            return ctx.enter_context(nc.psum_tensor(name, [P, 512], F32))

        work = [bank("work0"), bank("work1")]
        s_bank = [bank("s_first"), bank("s_second")]
        o_bank = [bank("o_first"), bank("o_second")]
        kv_bank = bank("kv_bank")
        tr_bank = bank("tr_bank")

        def w(name):
            return work[bank_of(name)]

        loaded = {n: sem(f"{n}_loaded") for n in ("wv", "wk", "wq", "wo", "small", "bias", "bcast")}
        x_loaded = sem("x_loaded")
        x_consumed = sem("x_consumed")
        ident_ready = sem("ident_ready")
        consts_ready = sem("consts_ready")
        ones_ready = sem("ones_ready")
        split_hi = sem("split_hi")
        split_done = sem("split_done")
        biasT_filled = sem("biasT_filled")
        bias_ready = sem("bias_ready")
        treeT_filled = sem("treeT_filled")
        treeT_ready = sem("treeT_ready")
        route_filled = sem("route_filled")
        route_hi = sem("route_hi")
        route_ready = sem("route_ready")
        pool_step = sem("pool_step")
        stats_step = sem("stats_step")
        moments_ready = sem("moments_ready")
        rstd_ready = sem("rstd_ready")
        xn_ready = sem("xn_ready")
        work_filled = [sem("work0_filled"), sem("work1_filled")]
        work_drained = [sem("work0_drained"), sem("work1_drained")]
        hi_ready = sem("hi_ready")
        relu_ready = sem("relu_ready")
        exp_ready = sem("exp_ready")
        k_hi = sem("k_hi")
        k_split_ready = sem("k_split_ready")
        q_zeroed = sem("q_zeroed")
        q_hi = sem("q_hi")
        q_split_ready = sem("q_split_ready")
        q_low_ready = sem("q_low_ready")
        k_tr_filled = sem("k_tr_filled")
        k_tok_ready = sem("k_tok_ready")
        s_filled = sem("s_filled")
        s_copied = sem("s_copied")
        a_masked = sem("a_masked")
        kv_filled = sem("kv_filled")
        snap_step = sem("snap_step")
        snap_ready = sem("snap_ready")
        state_ready = sem("state_ready")
        state_reset = sem("state_reset")
        o_filled = sem("o_filled")
        den_step = sem("den_step")
        o_normed = sem("o_normed")
        o_tr_filled = sem("o_tr_filled")
        oT_hi = sem("oT_hi")
        oT_ready = sem("oT_ready")
        leaf_step = sem("leaf_step")
        leaf_ready = sem("leaf_ready")
        y_stored = sem("y_stored")

        def wait_apart(eng, semaphore, value):
            if isinstance(value, int):
                eng.wait_ge(semaphore, value)
                return
            eng.reg_mov(scratch[eng.engine], value)
            eng.wait_ge(ident_ready, 1)
            eng.wait_ge(semaphore, scratch[eng.engine])

        def passes(lhs, rhs):
            return ((lhs(0), rhs(0)), (lhs(0), rhs(1)), (lhs(1), rhs(0)))

        SHARED = range(CH + 1, PAIRS)

        def lo_of_queries(eng, p, h):
            rows = slice(h * D, (h + 1) * D)
            return eng.tensor_tensor(q_split[rows, 1, :, h], qT[rows, p % 2].rearrange("p (c n) -> p c n", n=P),
                                     q_split[rows, 0, :, h].bitcast(F32), ALU.subtract)

        scratch = {eng.engine: eng.alloc_register("scratch") for eng in (nc.gpsimd, nc.vector, nc.tensor)}
        for eng in (nc.gpsimd, nc.vector, nc.tensor):
            eng.reg_mov(scratch[eng.engine], 0)

        block = ctx.enter_context(nc.Block())

        @block.sync
        def _(sp):
            sp.sem_inc(y_stored, AHEAD)
            sp.dma_start(x_in[:, :, :], x_rows[0]).then_inc(x_loaded, 16)
            for i, b in enumerate((bq, bk)):
                sp.dma_start(bias_rows[i * PAIRS:(i + 1) * PAIRS, :],
                             b.rearrange("(r n) -> r n", n=P)).then_inc(loaded["bias"], 16)
            for name, src in (("wv", Wv), ("wk", Wk), ("wq", Wq)):
                sp.dma_start(stage_of[name].rearrange("p (t n) -> p t n", t=KT_),
                             src.rearrange("(t p) n -> p t n", p=P)).then_inc(loaded[name], 16)
            sp.dma_start(bv_all[:, :], bv.partition_broadcast(P)).then_inc(loaded["bcast"], 16)
            sp.dma_start(y_bias[:, 0], bo.partition_broadcast(P)).then_inc(loaded["bcast"], 16)
            sp.dma_start(y_bias[:, 1], Wout_b.partition_broadcast(P)).then_inc(loaded["bcast"], 16)
            sp.wait_ge(consts_ready, 1)
            sp.dma_start(routers_in[:, 0], routers[0:P, :]).then_inc(loaded["small"], 16)
            sp.dma_start(routers_in[0:nodes - P, 1], routers[P:nodes, :]).then_inc(loaded["small"], 16)
            for dst, src in ((tree_wq_in, tree_Wq), (leaf_in, leaf_values), (wout_in, Wout_w)):
                sp.dma_start(dst, src.rearrange("(t p) n -> p t n", p=P)).then_inc(loaded["small"], 16)
            sp.wait_ge(split_done, 1)
            sp.dma_start(stage_of["wo"].rearrange("p (t n) -> p t n", t=PAIRS),
                         Wo.rearrange("(t p) n -> p t n", p=P)).then_inc(loaded["wo"], 16)

            def store(g):
                for i in range(2):
                    sp.wait_ge(work_drained[bank_of(f"y{i}")], count_of(f"y{i}", g))
                    sp.dma_start(out_rows[bass.ds(g, 1), :, 2 * i:2 * i + 2, :].rearrange("a p c d -> (a p) c d"),
                                 y_tile[:, 2 * i:2 * i + 2, :]).then_inc(y_stored, 16)

            last = batches * MACROS - 1
            with sp.Fori(0, last) as g:
                sp.wait_ge(x_consumed, g + 1)
                sp.dma_start(x_in[:, :, :], x_rows[bass.ds(g + 1, 1)].rearrange("a p c d -> (a p) c d"))\
                  .then_inc(x_loaded, 16)
                store(g)
            sp.wait_ge(x_consumed, last + 1)
            sp.dma_start(x_in[:, :, :], x_rows[0]).then_inc(x_loaded, 16)
            store(last)
            sp.wait_ge(y_stored, AHEAD + 32 * (last + 1))
            sp.wait_ge(x_loaded, 16 * (last + 2))

        @block.gpsimd
        def _(pool):
            pool.memset(routers_in[:, 1], 0.0).then_inc(consts_ready, 1)
            pool.memset(ident[:, :], 0.0).then_inc(pool_step, 1)
            pool.wait_ge(pool_step, 1)
            pool.affine_select(out=ident[:, :], in_=ident[:, :], compare_op=ALU.not_equal, fill=1.0, base=0,
                               pattern=[[-1, P]], channel_multiplier=1).then_inc(ident_ready, 1)
            pool.memset(minus_half[:, :], -0.5).then_inc(pool_step, 1)

            def ones(half):
                heads = v_aug[:, half].rearrange("p c (h e) -> p c h e", e=AUG)
                pool.memset(heads[:, :, :, D:AUG].rearrange("p c h e -> p c (h e)"), 1.0)\
                    .then_inc(ones_ready, 1)

            def inverse_deviation(count):
                wait_apart(pool, moments_ready, count)
                pool.tensor_scalar(rstd[:, :], mean_var[:, :, 1], EPS_NORM, None, ALU.add).then_inc(rstd_ready, 1)
                pool.wait_ge(rstd_ready, 2 * count - 1)
                pool.tensor_tensor(rstd[:, :], rstd[:, :], minus_half[:, :], ALU.pow).then_inc(rstd_ready, 1)

            pool.wait_ge(pool_step, 2)
            inverse_deviation(1)
            ones(0)
            pool.wait_ge(split_done, 3)
            ones(1)
            pool.wait_ge(treeT_ready, 3)
            pool.wait_ge(loaded["bcast"], 48)
            pool.tensor_tensor(y_bias[:, 0], y_bias[:, 0], y_bias[:, 1], ALU.add).then_inc(pool_step, 1)
            pool.wait_ge(pool_step, 3)

            LEVEL_STEPS = 2 * depth + 1

            def level(l, g):
                n = 1 << l
                bufs = (leaf_even, leaf_odd)
                src, dst = bufs[l % 2], bufs[(l + 1) % 2]
                kids = dst[:, :, 0:2 * n].rearrange("p c (n k) -> p c n k", k=2)
                left, right = kids[:, :, :, 0], kids[:, :, :, 1]
                g_l = gate[:, :, n - 1:2 * n - 1]
                wait_apart(pool, leaf_step, g * LEVEL_STEPS + 2 * l + 1)
                if l == 0:
                    pool.tensor_copy(right, g_l).then_inc(leaf_step, 1)
                    pool.tensor_scalar(left, g_l, -1.0, 1.0, ALU.mult, ALU.add).then_inc(leaf_step, 1)
                    return
                pool.tensor_tensor(right, src[:, :, 0:n], g_l, ALU.mult).then_inc(leaf_step, 1)
                pool.wait_ge(leaf_step, g * LEVEL_STEPS + 2 * l + 2)
                last = pool.tensor_tensor(left, src[:, :, 0:n], right, ALU.subtract)
                last.then_inc(leaf_step, 1)

            def unit(p, g):
                for i in range(2):
                    part = aT[:, 2 * i:2 * i + 2].rearrange("p c h n -> p (c h) n")
                    wait_apart(pool, s_copied, g * (2 * PAIRS) + (AHEAD + 2 * p + i + 1))
                    pool.affine_select(out=part, in_=part, compare_op=ALU.is_ge, fill=0.0, base=0,
                                       pattern=[[0, 4], [1, P]], channel_multiplier=-1).then_inc(a_masked, 1)
                if p == 0:
                    pool.wait_ge(work_drained[bank_of("y1")], count_before("y1", g))
                    pool.wait_ge(x_loaded, g * 16 + 16)
                    pool.tensor_tensor(resid, x_in[:, :, :],
                                       y_bias[:, 0].unsqueeze(1).to_broadcast([P, CH, hid]), ALU.add)\
                        .then_inc(x_consumed, 1)
                    for i in range(2):
                        wait_apart(pool, work_drained[bank_of(f"gate{i}")], count_before(f"gate{i}", g))
                    pool.tensor_scalar(gate, gate, 0.5, 0.5, ALU.mult, ALU.add).then_inc(leaf_step, 1)
                if p < CH:
                    for l in range(p * depth // CH, (p + 1) * depth // CH):
                        level(l, g)
                if p + 1 in SHARED:
                    pool.wait_ge(q_hi, g * PAIRS + (p + 2))
                    lo_of_queries(pool, p + 1, 0).then_inc(q_low_ready, 1)
                if p == CH:
                    inverse_deviation(g + 2)

            with pool.Fori(0, batches) as b:
                with pool.Fori(0, MACROS) as m:
                    g = pool.snap(b * MACROS + m)
                    for p in range(PAIRS):
                        unit(p, g)

        @block.scalar
        def _(act):
            def split(name, dst, count):
                act.wait_ge(loaded[name], 16)
                act.activation(dst[:, 0].rearrange("p t n -> p (t n)"), stage_of[name], ACT.Copy)\
                   .then_inc(split_hi, 1)

            def hi_of_work(name, count, dst, n_cols=TOK):
                act.wait_ge(work_filled[bank_of(name)], count)
                act.activation(dst, w(name)[:, 0:n_cols], ACT.Copy).then_inc(hi_ready, 1)

            def exponential(name, count, done):
                kind, p = name[0], int(name[1:])
                slot = 0 if kind == "K" else 1
                col = p + (PAIRS if kind == "K" else 0)
                act.wait_ge(work_filled[bank_of(name)], count)
                act.activation(ex[:, slot], w(name)[:, :], ACT.Relu, scale=-1.0, bias=neg_bias[:, col:col + 1])\
                   .then_inc(relu_ready, 1)
                act.wait_ge(relu_ready, done + 1)
                act.activation(ex[:, slot], ex[:, slot], ACT.Exp, scale=-1.0).then_inc(exp_ready, 1)

            def hi_of_k(p, drained):
                act.wait_ge(work_drained[bank_of(f"K{p}")], drained)
                act.activation(k_split[:, 0], kT[:, p % 2], ACT.Copy).then_inc(k_hi, 1)

            def hi_of_q(p, drained):
                act.wait_ge(work_drained[bank_of(f"Q{p}")], drained)
                for h in range(2):
                    rows = slice(h * D, (h + 1) * D)
                    last = act.activation(q_split[rows, 0, :, h], qT[rows, p % 2].rearrange("p (c n) -> p c n", n=P),
                                          ACT.Copy)
                last.then_inc(q_hi, 1)

            def half_gates(i, count):
                act.wait_ge(work_filled[bank_of(f"gate{i}")], count)
                act.activation(gate[:, 2 * i:2 * i + 2, :].rearrange("p c n -> p (c n)"), w(f"gate{i}")[:, :],
                               ACT.Tanh, scale=0.5).then_inc(work_drained[bank_of(f"gate{i}")], 1)

            def copy_oT(p, g):
                act.wait_ge(o_tr_filled, g * PAIRS + (p + 1))
                act.activation(oT[:, 0, p], tr_bank[:, :], ACT.Copy).then_inc(oT_hi, 1)

            act.sem_inc(s_copied, AHEAD)
            split("wv", wv, 1)
            for t in range(KT_):
                hi_of_work(f"xnT{t}", first_count(f"xnT{t}"), xnT[:, 0, t])
            split("wk", wk, 2)
            split("wq", wq, 3)
            act.wait_ge(bias_ready, 2)
            exponential("K0", first_count("K0"), 0)
            hi_of_k(0, first_count("K0"))
            for i, (src, dst) in enumerate(((s_bank[0], routersT), (s_bank[1], leafvT), (o_bank[0], woutT))):
                act.wait_ge(treeT_filled, i + 1)
                act.activation(dst.rearrange("p t n -> p (t n)"), src[:, :], ACT.Copy).then_inc(treeT_ready, 1)
            for i in range(LT):
                act.wait_ge(work_filled[1], first_count(f"tree_out{i}"))
                act.activation(tree_w[:, 0, i], work[1][:, 0:hid], ACT.Copy).then_inc(hi_ready, 1)
                if i == 0:
                    exponential("Q0", first_count("Q0"), 1)
            act.wait_ge(route_filled, 1)
            act.activation(route[:, 0].rearrange("p t n -> p (t n)"), kv_bank[:, :], ACT.Copy).then_inc(route_hi, 1)
            for i in range(2):
                half_gates(i, first_count(f"gate{i}"))
            split("wo", wo, 4)
            act.wait_ge(q_zeroed, 1)
            hi_of_q(0, first_count("Q0"))

            PHI = 2 * PAIRS

            def unit(p, g):
                act.wait_ge(k_tr_filled, g * PAIRS + (p + 1))
                act.activation(k_tok[:, :, :].rearrange("p c n -> p (c n)"), tr_bank[:, :], ACT.Copy)\
                   .then_inc(k_tok_ready, 1)
                if p < PAIRS - 1:
                    exponential(f"K{p + 1}", count_of(f"K{p + 1}", g), g * PHI + (2 + 2 * p))
                else:
                    for t in range(KT_):
                        hi_of_work(f"xnT{t}", count_of(f"xnT{t}", g), xnT[:, 0, t])
                if p > 0:
                    copy_oT(p - 1, g)
                for h in range(2):
                    act.wait_ge(s_filled, g * (2 * PAIRS) + (2 * p + h + 1))
                    act.activation(aT[:, 2 * h:2 * h + 2].rearrange("p c h n -> p (c h n)"), s_bank[h][:, :],
                                   ACT.Copy).then_inc(s_copied, 1)
                if p < PAIRS - 1:
                    hi_of_k(p + 1, count_of(f"K{p + 1}", g))
                if p < PAIRS - 1:
                    exponential(f"Q{p + 1}", count_of(f"Q{p + 1}", g), g * PHI + (3 + 2 * p))
                if CH <= p < CH + LT:
                    t = p - CH
                    hi_of_work(f"leafT{t}", count_of(f"leafT{t}", g), leafT[:, 0, t])
                if p < PAIRS - 1:
                    hi_of_q(p + 1, count_of(f"Q{p + 1}", g))

            with act.Fori(0, batches) as b:
                with act.Fori(0, MACROS) as m:
                    g = act.snap(b * MACROS + m)
                    for p in range(PAIRS):
                        unit(p, g)
                    copy_oT(PAIRS - 1, g)
                    exponential("K0", count_of("K0", g), g * PHI + (2 + 2 * (PAIRS - 1)))
                    hi_of_k(0, count_of("K0", g))
                    exponential("Q0", count_of("Q0", g), g * PHI + (3 + 2 * (PAIRS - 1)))
                    hi_of_q(0, count_of("Q0", g))
                    for i in range(2):
                        half_gates(i, count_of(f"gate{i}", g))

        @block.vector
        def _(dve):
            def layer_norm(count):
                dve.wait_ge(x_loaded, count * 16)
                for c in range(CH):
                    dve.bn_stats(stats[:, c], x_in[:, c]).then_inc(stats_step, 1)
                for c in range(CH):
                    wait_apart(dve, stats_step, count * CH + (c + 1 - CH))
                    last = dve.bn_aggr(mean_var[:, c], stats[:, c])
                last.then_inc(moments_ready, 1)

            def normalise(count):
                dve.wait_ge(moments_ready, count)
                dve.wait_ge(rstd_ready, 2 * count)
                for c in range(CH):
                    last = dve.tensor_scalar(xn[:, c], x_in[:, c], mean_var[:, c, 0:1], rstd[:, c:c + 1],
                                             ALU.subtract, ALU.mult)
                last.then_inc(xn_ready, 1)

            def split(name, dst, count):
                dve.wait_ge(split_hi, count)
                dve.tensor_tensor(dst[:, 1].rearrange("p t n -> p (t n)"), stage_of[name],
                                  dst[:, 0].bitcast(F32).rearrange("p t n -> p (t n)"), ALU.subtract)\
                   .then_inc(split_done, 1)

            def lo_of_work(name, dst, hi, done):
                dve.wait_ge(hi_ready, done)
                dve.tensor_tensor(dst, w(name)[:, :], hi.bitcast(F32), ALU.subtract)\
                   .then_inc(work_drained[bank_of(name)], 1)

            def phi(name, done):
                kind, p = name[0], int(name[1:])
                slot, dst = (0, kT) if kind == "K" else (1, qT)
                col = p + (PAIRS if kind == "K" else 0)
                dve.wait_ge(exp_ready, done)
                dve.scalar_tensor_tensor(out=dst[:, p % 2], in0=w(name)[:, :], scalar=bias_one[:, col:col + 1],
                                         in1=ex[:, slot], op0=ALU.add, op1=ALU.max)\
                   .then_inc(work_drained[bank_of(name)], 1)

            def lo_of_k(p, done):
                dve.wait_ge(k_hi, done)
                dve.tensor_tensor(k_split[:, 1], kT[:, p % 2], k_split[:, 0].bitcast(F32), ALU.subtract)\
                   .then_inc(k_split_ready, 1)

            def lo_of_q(p, done):
                dve.wait_ge(q_hi, done)
                last = lo_of_queries(dve, p, 1)
                if p not in SHARED:
                    last = lo_of_queries(dve, p, 0)
                last.then_inc(q_split_ready, 1)

            def values(name, count):
                half, c = int(name[1]), int(name[3:])
                n = 2 * HALF * D
                dst = v_aug[:, half, c].rearrange("p (h e) -> p h e", e=AUG)[:, :, 0:D]
                dve.wait_ge(work_filled[bank_of(name)], count)
                dve.tensor_tensor(dst, w(name)[:, :].rearrange("p (h e) -> p h e", e=D),
                                  bv_all[:, half * n:(half + 1) * n].rearrange("p (h e) -> p h e", e=D), ALU.add)\
                   .then_inc(work_drained[bank_of(name)], 1)

            for counter in (state_ready, o_normed, oT_ready):
                dve.sem_inc(counter, AHEAD)
            layer_norm(1)
            normalise(1)
            split("wv", wv, 1)
            dve.wait_ge(biasT_filled, 1)
            dve.tensor_scalar(neg_bias[:, :], tr_bank[:, 0:2 * PAIRS], -1.0, None, ALU.mult).then_inc(bias_ready, 1)
            dve.tensor_scalar(bias_one[:, :], tr_bank[:, 0:2 * PAIRS], 1.0, None, ALU.add).then_inc(bias_ready, 1)
            for t in range(KT_):
                lo_of_work(f"xnT{t}", xnT[:, 1, t], xnT[:, 0, t], t + 1)
            split("wk", wk, 2)
            dve.wait_ge(loaded["bcast"], 48)
            for c in range(2):
                values(f"V0c{c}", first_count(f"V0c{c}"))
            split("wq", wq, 3)
            for c in range(2, CH):
                values(f"V0c{c}", first_count(f"V0c{c}"))
            phi("K0", 1)
            lo_of_k(0, 1)
            for i in range(LT):
                dve.wait_ge(hi_ready, KT_ + i + 1)
                dve.tensor_tensor(tree_w[:, 1, i], work[1][:, 0:hid], tree_w[:, 0, i].bitcast(F32), ALU.subtract)\
                   .then_inc(work_drained[1], 1)
                if i == 0:
                    phi("Q0", 2)
            dve.wait_ge(route_hi, 1)
            dve.tensor_tensor(route[:, 1].rearrange("p t n -> p (t n)"), kv_bank[:, :],
                              route[:, 0].bitcast(F32).rearrange("p t n -> p (t n)"), ALU.subtract)\
               .then_inc(route_ready, 1)
            split("wo", wo, 4)
            dve.wait_ge(split_done, 4)
            dve.memset(q_split[:, :, :, :, :].bitcast(F32), 0.0).then_inc(q_zeroed, 1)
            lo_of_q(0, 1)
            dve.wait_ge(ones_ready, 2)

            HI_FIRST = KT_ + LT
            HI = KT_ + LT

            def add_state(c, before, after, step, sem_, inc):
                off = (c % 2) * 2 * AUG
                for h in range(2):
                    rows, cols = slice(h * D, (h + 1) * D), slice(h * AUG, (h + 1) * AUG)
                    last = dve.tensor_tensor(after[rows, cols], kv_bank[rows, off + h * AUG:off + (h + 1) * AUG],
                                             before[rows, cols], ALU.add)
                last.then_inc(sem_, inc)

            def norm(i, p, g):
                v = o_bank[i][:, 0:4 * AUG].rearrange("p (n e) -> p n e", e=AUG)
                n = 2 * p + i
                dve.wait_ge(o_filled, g * (2 * PAIRS) + (n + 1))
                dve.tensor_scalar(den[:, :], v[:, :, D], EPS_ATTN, None, ALU.add).then_inc(den_step, 1)
                dve.wait_ge(den_step, g * (4 * PAIRS) + (2 * n + 1))
                dve.reciprocal(rden[:, :], den[:, :]).then_inc(den_step, 1)
                dve.wait_ge(den_step, g * (4 * PAIRS) + (2 * n + 2))
                dst = o_tok[:, 2 * i:2 * i + 2].rearrange("p c (h e) -> p (c h) e", e=D)
                dve.tensor_tensor(dst, v[:, :, 0:D], rden[:, :].unsqueeze(2).to_broadcast([P, 4, D]), ALU.mult)\
                   .then_inc(o_normed, 1)

            def lo_of_oT(p, g):
                dve.wait_ge(oT_hi, g * PAIRS + (p + 1))
                dve.tensor_tensor(oT[:, 1, p], tr_bank[:, :], oT[:, 0, p].bitcast(F32), ALU.subtract)\
                   .then_inc(oT_ready, 1)

            PHI = 2 * PAIRS

            def unit(p, g):
                if p < PAIRS - 1:
                    phi(f"K{p + 1}", g * PHI + (2 + 2 * p + 1))
                else:
                    for t in range(KT_):
                        lo_of_work(f"xnT{t}", xnT[:, 1, t], xnT[:, 0, t], g * HI + (HI_FIRST + LT + t + 1))
                dve.wait_ge(kv_filled, g * (2 * PAIRS) + (2 * p + 1))
                add_state(0, state[:, p], snap[:, 0], 0, snap_step, 1)
                dve.wait_ge(snap_step, g * PAIRS + (p + 1))
                add_state(1, snap[:, 0], snap[:, 1], 1, snap_ready, 1)
                if p > 0:
                    lo_of_oT(p - 1, g)
                if p < PAIRS - 1:
                    lo_of_k(p + 1, g * PAIRS + (p + 2))
                dve.wait_ge(kv_filled, g * (2 * PAIRS) + (2 * p + 2))
                dve.wait_ge(snap_ready, g * (2 * PAIRS) + (2 * p + 1))
                add_state(2, snap[:, 1], snap[:, 2], 2, snap_ready, 1)
                if p < PAIRS - 1:
                    phi(f"Q{p + 1}", g * PHI + (2 + 2 * p + 2))
                else:
                    values("V0c0", count_of("V0c0", g))
                norm(0, p, g)
                dve.wait_ge(snap_ready, g * (2 * PAIRS) + (2 * p + 2))
                add_state(3, snap[:, 2], state[:, p], 3, state_ready, 1)
                if p < CH:
                    values(f"V1c{p}", count_of(f"V1c{p}", g))
                elif p < CH + LT:
                    t = p - CH
                    lo_of_work(f"leafT{t}", leafT[:, 1, t], leafT[:, 0, t], g * HI + (HI_FIRST + t + 1))
                if p < CH:
                    lo_of_q(p + 1, g * PAIRS + (p + 2))
                norm(1, p, g)
                if CH <= p < PAIRS - 1:
                    lo_of_q(p + 1, g * PAIRS + (p + 2))
                if p == CH:
                    layer_norm(g + 2)
                if p == CH + 1:
                    normalise(g + 2)

            with dve.Fori(0, batches) as b:
                dve.wait_ge(state_ready, b * (MACROS * PAIRS) + AHEAD)
                dve.memset(state[:, :, :], 0.0).then_inc(state_reset, 1)
                dve.wait_ge(state_reset, b * 2 + 1)
                dve.memset(snap[:, :, :], 0.0).then_inc(state_reset, 1)
                wait_apart(dve, state_reset, b * 2 + 2)
                with dve.Fori(0, MACROS) as m:
                    g = dve.snap(b * MACROS + m)
                    for p in range(PAIRS):
                        unit(p, g)
                    values("V0c1", count_of("V0c1", g))
                    lo_of_oT(PAIRS - 1, g)
                    for c in range(2, CH):
                        values(f"V0c{c}", count_of(f"V0c{c}", g))
                    dve.wait_ge(y_stored, g * 32 + AHEAD)
                    for i, kind in enumerate("KQ"):
                        phi(f"{kind}0", g * PHI + (2 + 2 * (PAIRS - 1) + i + 1))
                        (lo_of_k if kind == "K" else lo_of_q)(0, g * PAIRS + (PAIRS + 1))
                        name = f"y{i}"
                        dve.wait_ge(work_filled[bank_of(name)], count_of(name, g))
                        dve.tensor_tensor(y_tile[:, 2 * i:2 * i + 2], w(name)[:, :].rearrange("p (c d) -> p c d", d=hid),
                                          resid[:, 2 * i:2 * i + 2], ALU.add)\
                           .then_inc(work_drained[bank_of(name)], 1)

        @block.tensor
        def _(pe):
            def split_product(dst, lhs, rhs, tiles):
                steps = [s for t in range(tiles) for s in passes(lambda a, t=t: lhs(a, t), lambda a, t=t: rhs(a, t))]
                for i, (l, r) in enumerate(steps):
                    last = pe.matmul(dst, l, r, start=i == 0, stop=i == len(steps) - 1)
                return last

            def fill(name):
                dst = w(name) if name in FILLS else work[FIRST_FILLS.index(name) % 2]
                if name[0] in "KQ":
                    wt, p = (wk if name[0] == "K" else wq), int(name[1:])
                    return split_product(dst[:, :], lambda a, t: wt[:, a, t, p * P:(p + 1) * P],
                                         lambda a, t: xnT[:, a, t], KT_)
                if name[0] == "V":
                    half, c, n = int(name[1]), int(name[3:]), 2 * HALF * D
                    return split_product(dst[:, 0:n], lambda a, t: xnT[:, a, t, c * P:(c + 1) * P],
                                         lambda a, t: wv[:, a, t, half * n:(half + 1) * n], KT_)
                if name.startswith("xnT") or name.startswith("leafT"):
                    t, src = int(name[-1]), xn if name[0] == "x" else leaf_even
                    for c in range(CH):
                        last = pe.transpose(dst[:, c * P:(c + 1) * P], src[:, c, t * P:(t + 1) * P], ident[:, :])
                    return last
                if name.startswith("gate"):
                    i = int(name[-1])
                    for j in range(2):
                        c = 2 * i + j
                        last = split_product(dst[:, j * leaves:(j + 1) * leaves],
                                             lambda a, t: xnT[:, a, t, c * P:(c + 1) * P],
                                             lambda a, t: route[:, a, t], KT_)
                    return last
                if name.startswith("tree_out"):
                    i = int(name[-1])
                    for t in range(KT_):
                        last = pe.matmul(dst[:, 0:hid], leafvT[:, t, i * P:(i + 1) * P], woutT[:, t],
                                         start=t == 0, stop=t == KT_ - 1)
                    return last
                i = int(name[-1])
                for j in range(2):
                    c = 2 * i + j
                    cols = slice(c * P, (c + 1) * P)
                    last = split_product(dst[:, j * hid:(j + 1) * hid],
                                         lambda a, t: oT[:, a, t, cols] if t < PAIRS else leafT[:, a, t - PAIRS, cols],
                                         lambda a, t: wo[:, a, t] if t < PAIRS else tree_w[:, a, t - PAIRS],
                                         PAIRS + LT)
                return last

            def first_fill(name):
                i = FIRST_FILLS.index(name)
                if i >= 2:
                    pe.wait_ge(work_drained[i % 2], i // 2)
                fill(name).then_inc(work_filled[i % 2], 1)

            def loop_fill(name, g):
                pe.wait_ge(work_drained[bank_of(name)], g * PER_BANK + (FIRST_PER_BANK + FILLS.index(name) // 2))
                fill(name).then_inc(work_filled[bank_of(name)], 1)

            pe.wait_ge(ident_ready, 1)
            pe.wait_ge(loaded["bias"], 32)
            pe.transpose(tr_bank[:, 0:2 * PAIRS], bias_rows[:, :], ident[0:2 * PAIRS, 0:2 * PAIRS])\
              .then_inc(biasT_filled, 1)
            pe.wait_ge(xn_ready, 1)
            first_fill("xnT0")
            first_fill("xnT1")
            pe.wait_ge(split_done, 1)
            for c in range(CH):
                if c == 0:
                    pe.wait_ge(work_drained[1], 1)
                first_fill(f"V0c{c}")
            pe.wait_ge(split_done, 2)
            first_fill("K0")
            pe.wait_ge(loaded["small"], 80)
            for src, dst in ((routers_in, s_bank[0]), (leaf_in, s_bank[1]), (wout_in, o_bank[0])):
                v = dst[:, :].rearrange("p (t n) -> p t n", t=2)
                for i in range(2):
                    for j in range(2):
                        last = pe.transpose(v[:, i, j * P:(j + 1) * P], src[:, j, i * P:(i + 1) * P], ident[:, :])
                last.then_inc(treeT_filled, 1)
            pe.wait_ge(treeT_ready, 3)
            first_fill("tree_out0")
            pe.wait_ge(split_done, 3)
            first_fill("Q0")
            first_fill("tree_out1")
            for i in range(KT_):
                for t in range(KT_):
                    last = pe.matmul(kv_bank[:, i * leaves:(i + 1) * leaves], tree_wq_in[:, t, i * P:(i + 1) * P],
                                     routersT[:, t], start=t == 0, stop=t == KT_ - 1)
            last.then_inc(route_filled, 1)
            pe.wait_ge(route_ready, 1)
            first_fill("gate0")
            first_fill("gate1")
            pe.wait_ge(split_done, 4)

            def transpose_o(p, g):
                pe.wait_ge(o_normed, g * (2 * PAIRS) + (AHEAD + 2 * p + 2))
                pe.wait_ge(k_tok_ready, g * PAIRS + min(p + 2, PAIRS))
                for c in range(CH):
                    last = pe.transpose(tr_bank[:, c * P:(c + 1) * P], o_tok[:, c], ident[:, :])
                last.then_inc(o_tr_filled, 1)

            def outer_products(i, p, g):
                half, off = p // HALF, (p % HALF) * 2 * AUG
                for c in (2 * i, 2 * i + 1):
                    last = pe.matmul(kv_bank[:, (c % 2) * 2 * AUG:(c % 2 + 1) * 2 * AUG], k_tok[:, c],
                                     v_aug[:, half, c, off:off + 2 * AUG], start=True, stop=True)
                last.then_inc(kv_filled, 1)

            def attend(i, p, g):
                half = p // HALF
                for c in (2 * i, 2 * i + 1):
                    at = (c % 2) * 2 * AUG
                    before = state[:, p] if c == 0 else snap[:, c - 1]
                    pe.matmul(o_bank[i][:, at:at + 2 * AUG], qT[:, p % 2, c * P:(c + 1) * P], before,
                              start=True, stop=False)
                    for h in range(2):
                        off = (2 * (p % HALF) + h) * AUG
                        last = pe.matmul(o_bank[i][:, at + h * AUG:at + (h + 1) * AUG], aT[:, c, h],
                                         v_aug[:, half, c, off:off + AUG], start=False, stop=h == 1)
                last.then_inc(o_filled, 1)

            def unit(p, g):
                if p == 0:
                    pe.wait_ge(work_drained[bank_of("K0")], count_before("K0", g))
                    pe.wait_ge(oT_ready, g * PAIRS + AHEAD)
                elif p == 1:
                    pe.wait_ge(work_drained[bank_of("K1")], count_of("K1", g))
                    pe.wait_ge(k_tok_ready, g * PAIRS + 1)
                else:
                    pe.wait_ge(work_drained[bank_of(f"K{p}")], count_of(f"K{p}", g))
                    pe.wait_ge(oT_ready, g * PAIRS + (AHEAD + p - 1))
                for c in range(CH):
                    last = pe.transpose(tr_bank[:, c * P:(c + 1) * P], kT[:, p % 2, c * P:(c + 1) * P], ident[:, :])
                last.then_inc(k_tr_filled, 1)
                if p < PAIRS - 1:
                    loop_fill(f"K{p + 1}", g)
                else:
                    pe.wait_ge(xn_ready, g + 2)
                    loop_fill("xnT0", g)
                    loop_fill("xnT1", g)
                if p > 0:
                    transpose_o(p - 1, g)
                pe.wait_ge(k_split_ready, g * PAIRS + (p + 1))
                pe.wait_ge(q_split_ready, g * PAIRS + (p + 1))
                if p in SHARED:
                    pe.wait_ge(q_low_ready, g * len(SHARED) + (SHARED.index(p) + 1))
                pe.wait_ge(s_copied, g * (2 * PAIRS) + (AHEAD + 2 * p))
                for c in range(CH):
                    at = (c % 2) * 2 * P
                    last = split_product(s_bank[c // 2][:, at:at + 2 * P],
                                         lambda a, t: k_split[:, a, c * P:(c + 1) * P],
                                         lambda a, t: q_split[:, a, c].rearrange("p h n -> p (h n)"), 1)
                    if c % 2:
                        last.then_inc(s_filled, 1)
                if p == HALF:
                    pe.wait_ge(work_drained[bank_of("V1c3")], count_of("V1c3", g))
                    pe.wait_ge(work_drained[bank_of("V1c2")], count_of("V1c2", g))
                pe.wait_ge(k_tok_ready, g * PAIRS + (p + 1))
                pe.wait_ge(state_ready, g * PAIRS + (AHEAD + p))
                outer_products(0, p, g)
                if p < PAIRS - 1:
                    loop_fill(f"Q{p + 1}", g)
                else:
                    for t in range(KT_):
                        pe.wait_ge(work_drained[bank_of(f"xnT{t}")], count_of(f"xnT{t}", g))
                    loop_fill("V0c0", g)
                pe.wait_ge(snap_ready, g * (2 * PAIRS) + (2 * p + 1))
                outer_products(1, p, g)
                pe.wait_ge(a_masked, g * (2 * PAIRS) + (2 * p + 1))
                pe.wait_ge(o_normed, g * (2 * PAIRS) + (AHEAD + 2 * p))
                attend(0, p, g)
                if p < CH:
                    loop_fill(f"V1c{p}", g)
                elif p < CH + LT:
                    if p == CH:
                        pe.wait_ge(leaf_step, (g + 1) * (2 * depth + 1))
                    loop_fill(f"leafT{p - CH}", g)
                pe.wait_ge(a_masked, g * (2 * PAIRS) + (2 * p + 2))
                pe.wait_ge(snap_ready, g * (2 * PAIRS) + (2 * p + 2))
                attend(1, p, g)

            with pe.Fori(0, batches) as b:
                wait_apart(pe, state_reset, b * 2 + 2)
                with pe.Fori(0, MACROS) as m:
                    g = pe.snap(b * MACROS + m)
                    for p in range(PAIRS):
                        unit(p, g)
                    loop_fill("V0c1", g)
                    transpose_o(PAIRS - 1, g)
                    for name in ("V0c2", "V0c3", "K0"):
                        loop_fill(name, g)
                    pe.wait_ge(oT_ready, g * PAIRS + (AHEAD + PAIRS))
                    for name in ("y0", "Q0", "y1", "gate0", "gate1"):
                        loop_fill(name, g)


_INS = ['L0_attn_x', 'L0_attn_Wq', 'L0_attn_bq', 'L0_attn_Wk', 'L0_attn_bk', 'L0_attn_Wv', 'L0_attn_bv',
        'L0_attn_Wo', 'L0_attn_bo', 'L0_ffn_Wq', 'L0_ffn_routers', 'L0_ffn_leaf_keys', 'L0_ffn_leaf_values',
        'L0_ffn_Wout_w', 'L0_ffn_Wout_b']


def kernel(**inputs):
    import numpy as _np
    import concourse.bacc as _bacc
    from concourse import mybir as _mybir
    from concourse.bass_utils import run_bass_kernel_spmd as _run

    nc = _bacc.Bacc("TRN2", target_bir_lowering=False, num_devices=1)
    arrays, args = {}, []
    for name in _INS:
        a = _np.ascontiguousarray(inputs[name])
        arrays[f"in_{name}_dram"] = a
        args.append(nc.dram_tensor(f"in_{name}_dram", a.shape, _mybir.dt.from_np(a.dtype), kind="ExternalInput").ap())
    shape = inputs['L0_attn_x'].shape
    out = nc.dram_tensor("out_dram", shape, _mybir.dt.float32, kind="ExternalOutput").ap()
    attention_and_tree_layer(nc, *args, out)
    r = _run(nc, [arrays], core_ids=[0])
    return r.results[0]["out_dram"]
```

```python
from contextlib import ExitStack

import concourse.bass as bass
from concourse import mybir

ALU = mybir.AluOpType
ACT = mybir.ActivationFunctionType
F32 = mybir.dt.float32
F32R = mybir.dt.float32r

P = 128
HEADS, D = 16, 64
PAIRS = HEADS // 2
TOK = 512
CH = TOK // P
AUG = D + 1
HALF = PAIRS // 2
EPS_ATTN = 1e-6
EPS_NORM = 1e-5
AHEAD = 1

FIRST_FILLS = ["xnT0", "xnT1", "V0c0", "V0c1", "tree_out0", "V0c2", "K0", "V0c3", "Q0", "tree_out1", "gate0", "gate1"]
FILLS = []
for _p in range(PAIRS - 1):
    FILLS += [f"Q{_p + 1}", f"K{_p + 1}"]
    if _p < CH:
        FILLS.append(f"V1c{_p}")
    elif _p < CH + 2:
        FILLS.append(f"leafT{_p - CH}")
FILLS += ["xnT0", "xnT1"] + [f"V0c{c}" for c in range(CH)] + ["K0", "y0", "Q0", "y1", "gate0", "gate1"]
PER_BANK = len(FILLS) // 2
FIRST_PER_BANK = len(FIRST_FILLS) // 2
assert len(FILLS) % 2 == 0 and len(FIRST_FILLS) % 2 == 0


LAST_Y = ["V0c1", "V0c2"]


def bank_of(name):
    return FILLS.index(name) % 2


def count_of(name, g):
    return g * PER_BANK + (FIRST_PER_BANK + FILLS.index(name) // 2 + 1)


def count_before(name, g):
    return g * PER_BANK + (FIRST_PER_BANK + FILLS.index(name) // 2 + 1 - PER_BANK)


def first_count(name):
    return FIRST_FILLS.index(name) // 2 + 1


def attention_and_tree_layer(nc, x, Wq, bq, Wk, bk, Wv, bv, Wo, bo,
                             tree_Wq, routers, leaf_keys, leaf_values, Wout_w, Wout_b, out):
    batches, seq, hid = x.shape
    KT_ = hid // P
    MACROS = seq // TOK
    inner = HEADS * D
    leaves = leaf_values.shape[0]
    nodes = routers.shape[0]
    depth = leaves.bit_length() - 1
    LT = leaves // P
    final = batches * MACROS - 1
    assert KT_ == 2 and LT == 2 and nodes == leaves - 1 and Wq.shape[1] == inner

    x_rows = x.rearrange("b (t c p) d -> (b t) p c d", c=CH, p=P)
    out_rows = out.rearrange("b (t c p) d -> (b t) p c d", c=CH, p=P)

    with ExitStack() as ctx:
        def sb(name, shape, dt=F32):
            return ctx.enter_context(nc.sbuf_tensor(name, shape, dt))

        def sem(name):
            return ctx.enter_context(nc.semaphore(name))

        wq = sb("wq", [P, 2, KT_, inner], F32R)
        wk = sb("wk", [P, 2, KT_, inner], F32R)
        wv = sb("wv", [P, 2, KT_, inner], F32R)
        wo = sb("wo", [P, 2, PAIRS, hid], F32R)
        route = sb("route", [P, 2, KT_, leaves], F32R)
        tree_w = sb("tree_w", [P, 2, LT, hid], F32R)

        ident = sb("ident", [P, P])
        bias_rows = sb("bias_rows", [2 * PAIRS, P])
        neg_bias = sb("neg_bias", [P, 2 * PAIRS])
        bias_one = sb("bias_one", [P, 2 * PAIRS])
        bv_all = sb("bv_all", [P, inner])
        y_bias = sb("y_bias", [P, 2, hid])
        minus_half = sb("minus_half", [P, CH])

        x_in = sb("x_in", [P, CH, hid])
        y_buf = sb("y_buf", [P, 2, CH, hid])
        resid, y_tile = y_buf[:, 0], y_buf[:, 1]
        xn = sb("xn", [P, CH, hid])
        stats = sb("stats", [P, CH, 6])
        mean_var = sb("mean_var", [P, CH, 2])
        rstd = sb("rstd", [P, CH])
        xnT = sb("xnT", [P, 2, KT_, TOK], F32R)
        v_aug = sb("v_aug", [P, 2, CH, 2 * HALF * AUG])
        ffn_tok = sb("ffn_tok", [P, CH * leaves * 2 + CH * leaves // 2])
        gate = ffn_tok[:, 0:CH * leaves].rearrange("p (c n) -> p c n", c=CH)
        leaf_even = ffn_tok[:, CH * leaves:2 * CH * leaves].rearrange("p (c n) -> p c n", c=CH)
        leaf_odd = ffn_tok[:, 2 * CH * leaves:].rearrange("p (c n) -> p c n", c=CH)
        leafT = sb("leafT", [P, 2, LT, TOK], F32R)
        oT = sb("oT", [P, 2, PAIRS, TOK], F32R)

        kT = sb("kT", [P, 2, TOK])
        qT = sb("qT", [P, 2, TOK])
        ex = sb("ex", [P, 2, TOK])
        k_tok = sb("k_tok", [P, CH, P])
        k_split = sb("k_split", [P, 2, TOK], F32R)
        aT = sb("aT", [P, CH, 2, P])
        state = sb("state", [P, PAIRS, 2 * AUG])
        snap = sb("snap", [P, CH - 1, 2 * AUG])
        o_tok = sb("o_tok", [P, CH, P])
        den = sb("den", [P, 4])
        rden = sb("rden", [P, 4])
        with nc.sbuf_tensor("stage0", [P, KT_ * inner], F32) as stage0:
            pass
        q_split = sb("q_split", [P, 2, CH, 2, P], F32R)

        y_stage = y_buf[:, :, :, :].rearrange("p a c d -> p (a c d)")
        v_stage = v_aug[:, 1].rearrange("p c n -> p (c n)")[:, 0:KT_ * inner]

        def weight_halves(weights, stage, tiles, source):
            staged = stage.rearrange("p (t n) -> p t n", t=tiles)
            source = source.rearrange("(t p) n -> p t n", p=P)
            if tiles == KT_:
                at = [(slice(None), slice(None), slice(i * inner // 2, (i + 1) * inner // 2)) for i in range(2)]
            else:
                at = [(slice(None), slice(i * tiles // 2, (i + 1) * tiles // 2), slice(None)) for i in range(2)]
            return [(source[a], staged[a], weights[:, 0][a], weights[:, 1][a]) for a in at]

        halves = {}
        for name, weights, stage, tiles, source in (("wv", wv, stage0[:, :], KT_, Wv), ("wk", wk, y_stage, KT_, Wk),
                                                    ("wq", wq, v_stage, KT_, Wq), ("wo", wo, y_stage, PAIRS, Wo)):
            for i, parts in enumerate(weight_halves(weights, stage, tiles, source)):
                halves[f"{name}{i}"] = parts
        HI_ORDER = ["wv0", "wv1", "wk0", "wk1", "wq0", "wq1", "wo0", "wo1"]
        LO_VECTOR = ["wv0", "wk0", "wq0", "wo0", "wo1"]
        LO_POOL = ["wv1", "wk1", "wq1"]
        small = [ffn_tok[:, i * 2 * hid:(i + 1) * 2 * hid].rearrange("p (t n) -> p t n", t=2) for i in range(4)]
        routers_in, tree_wq_in, leaf_in, wout_in = small
        routersT = aT[:, 0:2].rearrange("p c h n -> p (c h n)").rearrange("p (t n) -> p t n", t=2)
        leafvT = aT[:, 2:4].rearrange("p c h n -> p (c h n)").rearrange("p (t n) -> p t n", t=2)
        woutT = k_tok[:, :, :].rearrange("p c n -> p (c n)").rearrange("p (t n) -> p t n", t=2)

        def bank(name):
            return ctx.enter_context(nc.psum_tensor(name, [P, 512], F32))

        work = [bank("work0"), bank("work1")]
        s_bank = [bank("s_first"), bank("s_second")]
        o_bank = [bank("o_first"), bank("o_second")]
        kv_bank = bank("kv_bank")
        tr_bank = bank("tr_bank")

        def w(name):
            return work[bank_of(name)]

        loaded = {n: sem(f"{n}_loaded") for n in ("wv0", "wv1", "wk0", "wk1", "wq0", "wq1", "wo0", "wo1",
                                                  "small", "bias", "bv", "y_bias")}
        x_loaded = sem("x_loaded")
        x_consumed = sem("x_consumed")
        ident_ready = sem("ident_ready")
        consts_ready = sem("consts_ready")
        ones_ready = sem("ones_ready")
        split_hi = sem("split_hi")
        split_lo = sem("split_lo")
        split_lo_pool = sem("split_lo_pool")
        biasT_filled = sem("biasT_filled")
        bias_ready = sem("bias_ready")
        treeT_filled = sem("treeT_filled")
        treeT_ready = sem("treeT_ready")
        route_filled = sem("route_filled")
        route_hi = sem("route_hi")
        route_ready = sem("route_ready")
        pool_step = sem("pool_step")
        stats_step = sem("stats_step")
        moments_ready = sem("moments_ready")
        rstd_ready = sem("rstd_ready")
        xn_ready = sem("xn_ready")
        work_filled = [sem("work0_filled"), sem("work1_filled")]
        work_drained = [sem("work0_drained"), sem("work1_drained")]
        hi_ready = sem("hi_ready")
        relu_ready = sem("relu_ready")
        exp_ready = sem("exp_ready")
        k_hi = sem("k_hi")
        k_split_ready = sem("k_split_ready")
        q_zeroed = sem("q_zeroed")
        q_hi = sem("q_hi")
        q_split_ready = sem("q_split_ready")
        q_low_ready = sem("q_low_ready")
        k_low_ready = sem("k_low_ready")
        k_tr_filled = sem("k_tr_filled")
        k_tok_ready = sem("k_tok_ready")
        s_filled = sem("s_filled")
        s_copied = sem("s_copied")
        a_masked = sem("a_masked")
        kv_filled = sem("kv_filled")
        snap_step = sem("snap_step")
        snap_ready = sem("snap_ready")
        state_ready = sem("state_ready")
        state_reset = sem("state_reset")
        snap_zeroed = sem("snap_zeroed")
        o_filled = sem("o_filled")
        den_step = sem("den_step")
        o_normed = sem("o_normed")
        o_tr_filled = sem("o_tr_filled")
        oT_hi = sem("oT_hi")
        oT_ready = sem("oT_ready")
        leaf_step = sem("leaf_step")
        leaf_ready = sem("leaf_ready")
        y_stored = sem("y_stored")

        def wait_apart(eng, semaphore, value):
            if isinstance(value, int):
                eng.wait_ge(semaphore, value)
                return
            eng.reg_mov(scratch[eng.engine], value)
            eng.wait_ge(ident_ready, 1)
            eng.wait_ge(semaphore, scratch[eng.engine])

        def passes(lhs, rhs):
            return ((lhs(0), rhs(0)), (lhs(0), rhs(1)), (lhs(1), rhs(0)))

        SHARED = range(CH + 1, PAIRS)

        def lo_of_keys(eng, p, cols):
            return eng.tensor_tensor(k_split[:, 1, cols], kT[:, p % 2, cols], k_split[:, 0, cols].bitcast(F32),
                                     ALU.subtract)

        def lo_of_queries(eng, p, h):
            rows = slice(h * D, (h + 1) * D)
            return eng.tensor_tensor(q_split[rows, 1, :, h], qT[rows, p % 2].rearrange("p (c n) -> p c n", n=P),
                                     q_split[rows, 0, :, h].bitcast(F32), ALU.subtract)

        def split_low(eng, name, done):
            _, stage, hi, lo = halves[name]
            eng.wait_ge(split_hi, HI_ORDER.index(name) + 1)
            eng.tensor_tensor(lo, stage, hi.bitcast(F32), ALU.subtract).then_inc(done, 1)

        scratch = {eng.engine: eng.alloc_register("scratch") for eng in (nc.gpsimd, nc.vector, nc.tensor)}
        for eng in (nc.gpsimd, nc.vector, nc.tensor):
            eng.reg_mov(scratch[eng.engine], 0)

        block = ctx.enter_context(nc.Block())

        @block.sync
        def _(sp):
            sp.sem_inc(y_stored, AHEAD)
            sp.dma_start(x_in[:, :, :], x_rows[0]).then_inc(x_loaded, 16)
            for i, b in enumerate((bq, bk)):
                sp.dma_start(bias_rows[i * PAIRS:(i + 1) * PAIRS, :],
                             b.rearrange("(r n) -> r n", n=P)).then_inc(loaded["bias"], 16)
            sp.wait_ge(consts_ready, 1)
            sp.dma_start(routers_in[:, 0], routers[0:P, :]).then_inc(loaded["small"], 16)
            sp.dma_start(routers_in[0:nodes - P, 1], routers[P:nodes, :]).then_inc(loaded["small"], 16)
            for dst, src in ((tree_wq_in, tree_Wq), (leaf_in, leaf_values), (wout_in, Wout_w)):
                sp.dma_start(dst, src.rearrange("(t p) n -> p t n", p=P)).then_inc(loaded["small"], 16)

            def load(name):
                source, stage, _, _ = halves[name]
                sp.dma_start(stage, source).then_inc(loaded[name], 16)

            load("wv0")
            load("wv1")
            sp.dma_start(bv_all[:, :], bv.partition_broadcast(P)).then_inc(loaded["bv"], 16)
            for name in ("wk0", "wk1", "wq0", "wq1"):
                load(name)
            sp.dma_start(y_bias[:, 0], bo.partition_broadcast(P)).then_inc(loaded["y_bias"], 16)
            sp.dma_start(y_bias[:, 1], Wout_b.partition_broadcast(P)).then_inc(loaded["y_bias"], 16)
            sp.wait_ge(split_lo, LO_VECTOR.index("wk0") + 1)
            sp.wait_ge(split_lo_pool, LO_POOL.index("wk1") + 1)
            load("wo0")
            load("wo1")

            def store(g, fills=("y0", "y1")):
                for i in range(2):
                    sp.wait_ge(work_drained[bank_of(fills[i])], count_of(fills[i], g))
                    sp.dma_start(out_rows[bass.ds(g, 1), :, 2 * i:2 * i + 2, :].rearrange("a p c d -> (a p) c d"),
                                 y_tile[:, 2 * i:2 * i + 2, :]).then_inc(y_stored, 16)

            with sp.Fori(0, final) as g:
                sp.wait_ge(x_consumed, g + 1)
                sp.dma_start(x_in[:, :, :], x_rows[bass.ds(g + 1, 1)].rearrange("a p c d -> (a p) c d"))\
                  .then_inc(x_loaded, 16)
                store(g)
            sp.wait_ge(x_consumed, final + 1)
            sp.dma_start(x_in[:, :, :], x_rows[0]).then_inc(x_loaded, 16)
            store(final, LAST_Y)
            sp.wait_ge(y_stored, AHEAD + 32 * (final + 1))
            sp.wait_ge(x_loaded, 16 * (final + 2))

        @block.gpsimd
        def _(pool):
            pool.memset(routers_in[:, 1], 0.0).then_inc(consts_ready, 1)
            pool.memset(ident[:, :], 0.0).then_inc(pool_step, 1)
            pool.wait_ge(pool_step, 1)
            pool.affine_select(out=ident[:, :], in_=ident[:, :], compare_op=ALU.not_equal, fill=1.0, base=0,
                               pattern=[[-1, P]], channel_multiplier=1).then_inc(ident_ready, 1)
            pool.memset(minus_half[:, :], -0.5).then_inc(pool_step, 1)

            def ones(half):
                heads = v_aug[:, half].rearrange("p c (h e) -> p c h e", e=AUG)
                pool.memset(heads[:, :, :, D:AUG].rearrange("p c h e -> p c (h e)"), 1.0)\
                    .then_inc(ones_ready, 1)

            def inverse_deviation(count):
                wait_apart(pool, moments_ready, count)
                pool.tensor_scalar(rstd[:, :], mean_var[:, :, 1], EPS_NORM, None, ALU.add).then_inc(rstd_ready, 1)
                pool.wait_ge(rstd_ready, 2 * count - 1)
                pool.tensor_tensor(rstd[:, :], rstd[:, :], minus_half[:, :], ALU.pow).then_inc(rstd_ready, 1)

            pool.wait_ge(pool_step, 2)
            inverse_deviation(1)
            ones(0)
            pool.memset(snap[:, :, :], 0.0).then_inc(snap_zeroed, 1)
            split_low(pool, "wv1", split_lo_pool)
            pool.wait_ge(split_lo_pool, 1)
            pool.wait_ge(split_lo, 1)
            pool.memset(q_split[:, :, :, :, :].bitcast(F32), 0.0).then_inc(q_zeroed, 1)
            split_low(pool, "wk1", split_lo_pool)
            split_low(pool, "wq1", split_lo_pool)
            pool.wait_ge(split_lo_pool, 3)
            pool.wait_ge(split_lo, LO_VECTOR.index("wq0") + 1)
            ones(1)
            pool.wait_ge(loaded["y_bias"], 32)
            pool.tensor_tensor(y_bias[:, 0], y_bias[:, 0], y_bias[:, 1], ALU.add).then_inc(pool_step, 1)
            pool.wait_ge(pool_step, 3)

            LEVEL_STEPS = 2 * depth + 1

            def level(l, g):
                n = 1 << l
                bufs = (leaf_even, leaf_odd)
                src, dst = bufs[l % 2], bufs[(l + 1) % 2]
                kids = dst[:, :, 0:2 * n].rearrange("p c (n k) -> p c n k", k=2)
                left, right = kids[:, :, :, 0], kids[:, :, :, 1]
                g_l = gate[:, :, n - 1:2 * n - 1]
                wait_apart(pool, leaf_step, g * LEVEL_STEPS + 2 * l + 1)
                if l == 0:
                    pool.tensor_copy(right, g_l).then_inc(leaf_step, 1)
                    pool.tensor_scalar(left, g_l, -1.0, 1.0, ALU.mult, ALU.add).then_inc(leaf_step, 1)
                    return
                pool.tensor_tensor(right, src[:, :, 0:n], g_l, ALU.mult).then_inc(leaf_step, 1)
                pool.wait_ge(leaf_step, g * LEVEL_STEPS + 2 * l + 2)
                last = pool.tensor_tensor(left, src[:, :, 0:n], right, ALU.subtract)
                last.then_inc(leaf_step, 1)

            def unit(p, g):
                for i in range(2):
                    part = aT[:, 2 * i:2 * i + 2].rearrange("p c h n -> p (c h) n")
                    wait_apart(pool, s_copied, g * (2 * PAIRS) + (AHEAD + 2 * p + i + 1))
                    pool.affine_select(out=part, in_=part, compare_op=ALU.is_ge, fill=0.0, base=0,
                                       pattern=[[0, 4], [1, P]], channel_multiplier=-1).then_inc(a_masked, 1)
                if p == 0:
                    pool.wait_ge(split_lo, len(LO_VECTOR))
                    pool.wait_ge(work_drained[bank_of("y1")], count_before("y1", g))
                    pool.wait_ge(x_loaded, g * 16 + 16)
                    pool.tensor_tensor(resid, x_in[:, :, :],
                                       y_bias[:, 0].unsqueeze(1).to_broadcast([P, CH, hid]), ALU.add)\
                        .then_inc(x_consumed, 1)
                    for i in range(2):
                        wait_apart(pool, work_drained[bank_of(f"gate{i}")], count_before(f"gate{i}", g))
                    pool.tensor_scalar(gate, gate, 0.5, 0.5, ALU.mult, ALU.add).then_inc(leaf_step, 1)
                if p < CH:
                    for l in range(p * depth // CH, (p + 1) * depth // CH):
                        level(l, g)
                if p + 1 in SHARED:
                    pool.wait_ge(q_hi, g * (2 * PAIRS) + (2 * p + 3))
                    lo_of_queries(pool, p + 1, 0).then_inc(q_low_ready, 1)
                    pool.wait_ge(k_hi, g * PAIRS + (p + 2))
                    lo_of_keys(pool, p + 1, slice(TOK // 2, TOK)).then_inc(k_low_ready, 1)
                if p == CH:
                    inverse_deviation(g + 2)

            with pool.Fori(0, batches) as b:
                wait_apart(pool, state_ready, b * (MACROS * PAIRS) + AHEAD)
                pool.memset(state[:, :, :], 0.0).then_inc(state_reset, 1)
                with pool.Fori(0, MACROS) as m:
                    g = pool.snap(b * MACROS + m)
                    for p in range(PAIRS):
                        unit(p, g)

        @block.scalar
        def _(act):
            def split_high(name):
                _, stage, hi, _ = halves[name]
                act.wait_ge(loaded[name], 16)
                act.activation(hi, stage, ACT.Copy).then_inc(split_hi, 1)

            def tree_w_high(i):
                bank = FIRST_FILLS.index(f"tree_out{i}") % 2
                act.wait_ge(work_filled[bank], first_count(f"tree_out{i}"))
                act.activation(tree_w[:, 0, i], work[bank][:, 0:hid], ACT.Copy).then_inc(hi_ready, 1)

            def copy_treeT(i):
                src, dst = ((s_bank[0], routersT), (s_bank[1], leafvT), (o_bank[0], woutT))[i]
                act.wait_ge(treeT_filled, i + 1)
                act.activation(dst.rearrange("p t n -> p (t n)"), src[:, :], ACT.Copy).then_inc(treeT_ready, 1)

            def hi_of_work(name, count, dst, n_cols=TOK):
                act.wait_ge(work_filled[bank_of(name)], count)
                act.activation(dst, w(name)[:, 0:n_cols], ACT.Copy).then_inc(hi_ready, 1)

            def exponential(name, count, done):
                kind, p = name[0], int(name[1:])
                slot = 0 if kind == "K" else 1
                col = p + (PAIRS if kind == "K" else 0)
                act.wait_ge(work_filled[bank_of(name)], count)
                act.activation(ex[:, slot], w(name)[:, :], ACT.Relu, scale=-1.0, bias=neg_bias[:, col:col + 1])\
                   .then_inc(relu_ready, 1)
                act.wait_ge(relu_ready, done + 1)
                act.activation(ex[:, slot], ex[:, slot], ACT.Exp, scale=-1.0).then_inc(exp_ready, 1)

            def hi_of_k(p, drained):
                act.wait_ge(work_drained[bank_of(f"K{p}")], drained)
                act.activation(k_split[:, 0], kT[:, p % 2], ACT.Copy).then_inc(k_hi, 1)

            def hi_of_q(p, drained):
                act.wait_ge(work_drained[bank_of(f"Q{p}")], drained)
                for h in range(2):
                    rows = slice(h * D, (h + 1) * D)
                    act.activation(q_split[rows, 0, :, h], qT[rows, p % 2].rearrange("p (c n) -> p c n", n=P),
                                   ACT.Copy).then_inc(q_hi, 1)

            def half_gates(i, count):
                act.wait_ge(work_filled[bank_of(f"gate{i}")], count)
                act.activation(gate[:, 2 * i:2 * i + 2, :].rearrange("p c n -> p (c n)"), w(f"gate{i}")[:, :],
                               ACT.Tanh, scale=0.5).then_inc(work_drained[bank_of(f"gate{i}")], 1)

            def copy_oT(p, g):
                act.wait_ge(o_tr_filled, g * PAIRS + (p + 1))
                act.activation(oT[:, 0, p], tr_bank[:, :], ACT.Copy).then_inc(oT_hi, 1)

            act.sem_inc(s_copied, AHEAD)
            copy_treeT(0)
            split_high("wv0")
            for t in range(KT_):
                hi_of_work(f"xnT{t}", first_count(f"xnT{t}"), xnT[:, 0, t])
            split_high("wv1")
            act.wait_ge(route_filled, 1)
            act.activation(route[:, 0].rearrange("p t n -> p (t n)"), kv_bank[:, :], ACT.Copy).then_inc(route_hi, 1)
            copy_treeT(1)
            copy_treeT(2)
            split_high("wk0")
            split_high("wk1")
            tree_w_high(0)
            split_high("wq0")
            split_high("wq1")
            act.wait_ge(bias_ready, 2)
            exponential("K0", first_count("K0"), 0)
            hi_of_k(0, first_count("K0"))
            exponential("Q0", first_count("Q0"), 1)
            tree_w_high(1)
            split_high("wo0")
            act.wait_ge(q_zeroed, 1)
            hi_of_q(0, first_count("Q0"))
            split_high("wo1")
            for i in range(2):
                half_gates(i, first_count(f"gate{i}"))

            PHI = 2 * PAIRS

            def unit(p, g):
                act.wait_ge(k_tr_filled, g * PAIRS + (p + 1))
                act.activation(k_tok[:, :, :].rearrange("p c n -> p (c n)"), tr_bank[:, :], ACT.Copy)\
                   .then_inc(k_tok_ready, 1)
                if p < PAIRS - 1:
                    exponential(f"Q{p + 1}", count_of(f"Q{p + 1}", g), g * PHI + (2 + 2 * p))
                else:
                    for t in range(KT_):
                        hi_of_work(f"xnT{t}", count_of(f"xnT{t}", g), xnT[:, 0, t])
                if p > 0:
                    copy_oT(p - 1, g)
                for h in range(2):
                    act.wait_ge(s_filled, g * (2 * PAIRS) + (2 * p + h + 1))
                    act.activation(aT[:, 2 * h:2 * h + 2].rearrange("p c h n -> p (c h n)"), s_bank[h][:, :],
                                   ACT.Copy).then_inc(s_copied, 1)
                if p < PAIRS - 1:
                    hi_of_q(p + 1, count_of(f"Q{p + 1}", g))
                    exponential(f"K{p + 1}", count_of(f"K{p + 1}", g), g * PHI + (3 + 2 * p))
                if CH <= p < CH + LT:
                    t = p - CH
                    hi_of_work(f"leafT{t}", count_of(f"leafT{t}", g), leafT[:, 0, t])
                if p < PAIRS - 1:
                    hi_of_k(p + 1, count_of(f"K{p + 1}", g))

            with act.Fori(0, batches) as b:
                with act.Fori(0, MACROS) as m:
                    g = act.snap(b * MACROS + m)
                    for p in range(PAIRS):
                        unit(p, g)
                    copy_oT(PAIRS - 1, g)
                    with act.If(g < final):
                        exponential("K0", count_of("K0", g), g * PHI + (2 + 2 * (PAIRS - 1)))
                        hi_of_k(0, count_of("K0", g))
                        exponential("Q0", count_of("Q0", g), g * PHI + (3 + 2 * (PAIRS - 1)))
                        hi_of_q(0, count_of("Q0", g))
                        for i in range(2):
                            half_gates(i, count_of(f"gate{i}", g))

        @block.vector
        def _(dve):
            def layer_norm(count):
                dve.wait_ge(x_loaded, count * 16)
                for c in range(CH):
                    dve.bn_stats(stats[:, c], x_in[:, c]).then_inc(stats_step, 1)
                for c in range(CH):
                    wait_apart(dve, stats_step, count * CH + (c + 1 - CH))
                    last = dve.bn_aggr(mean_var[:, c], stats[:, c])
                last.then_inc(moments_ready, 1)

            def normalise(count):
                dve.wait_ge(moments_ready, count)
                dve.wait_ge(rstd_ready, 2 * count)
                for c in range(CH):
                    last = dve.tensor_scalar(xn[:, c], x_in[:, c], mean_var[:, c, 0:1], rstd[:, c:c + 1],
                                             ALU.subtract, ALU.mult)
                last.then_inc(xn_ready, 1)

            def lo_of_work(name, dst, hi, done):
                dve.wait_ge(hi_ready, done)
                dve.tensor_tensor(dst, w(name)[:, :], hi.bitcast(F32), ALU.subtract)\
                   .then_inc(work_drained[bank_of(name)], 1)

            def phi(name, done):
                kind, p = name[0], int(name[1:])
                slot, dst = (0, kT) if kind == "K" else (1, qT)
                col = p + (PAIRS if kind == "K" else 0)
                dve.wait_ge(exp_ready, done)
                dve.scalar_tensor_tensor(out=dst[:, p % 2], in0=w(name)[:, :], scalar=bias_one[:, col:col + 1],
                                         in1=ex[:, slot], op0=ALU.add, op1=ALU.max)\
                   .then_inc(work_drained[bank_of(name)], 1)

            def lo_of_k(p, done):
                dve.wait_ge(k_hi, done)
                lo_of_keys(dve, p, slice(0, TOK // 2 if p in SHARED else TOK)).then_inc(k_split_ready, 1)

            def lo_of_q(p, done):
                dve.wait_ge(q_hi, done * 2)
                last = lo_of_queries(dve, p, 1)
                if p not in SHARED:
                    last = lo_of_queries(dve, p, 0)
                last.then_inc(q_split_ready, 1)

            def values(name, count, bank=None):
                half, c = int(name[1]), int(name[3:])
                n = 2 * HALF * D
                dst = v_aug[:, half, c].rearrange("p (h e) -> p h e", e=AUG)[:, :, 0:D]
                bank = bank_of(name) if bank is None else bank
                dve.wait_ge(work_filled[bank], count)
                dve.tensor_tensor(dst, work[bank][:, :].rearrange("p (h e) -> p h e", e=D),
                                  bv_all[:, half * n:(half + 1) * n].rearrange("p (h e) -> p h e", e=D), ALU.add)\
                   .then_inc(work_drained[bank], 1)

            def first_values(name):
                values(name, first_count(name), FIRST_FILLS.index(name) % 2)

            def tree_w_low(i):
                bank = FIRST_FILLS.index(f"tree_out{i}") % 2
                dve.wait_ge(hi_ready, KT_ + i + 1)
                dve.tensor_tensor(tree_w[:, 1, i], work[bank][:, 0:hid], tree_w[:, 0, i].bitcast(F32), ALU.subtract)\
                   .then_inc(work_drained[bank], 1)

            for counter in (state_ready, o_normed, oT_ready):
                dve.sem_inc(counter, AHEAD)
            layer_norm(1)
            normalise(1)
            split_low(dve, "wv0", split_lo)
            dve.wait_ge(biasT_filled, 1)
            dve.tensor_scalar(neg_bias[:, :], tr_bank[:, 0:2 * PAIRS], -1.0, None, ALU.mult).then_inc(bias_ready, 1)
            dve.tensor_scalar(bias_one[:, :], tr_bank[:, 0:2 * PAIRS], 1.0, None, ALU.add).then_inc(bias_ready, 1)
            for t in range(KT_):
                lo_of_work(f"xnT{t}", xnT[:, 1, t], xnT[:, 0, t], t + 1)
            dve.wait_ge(route_hi, 1)
            dve.tensor_tensor(route[:, 1].rearrange("p t n -> p (t n)"), kv_bank[:, :],
                              route[:, 0].bitcast(F32).rearrange("p t n -> p (t n)"), ALU.subtract)\
               .then_inc(route_ready, 1)
            dve.wait_ge(loaded["bv"], 16)
            first_values("V0c0")
            first_values("V0c1")
            split_low(dve, "wk0", split_lo)
            tree_w_low(0)
            first_values("V0c2")
            split_low(dve, "wq0", split_lo)
            phi("K0", 1)
            first_values("V0c3")
            lo_of_k(0, 1)
            phi("Q0", 2)
            tree_w_low(1)
            split_low(dve, "wo0", split_lo)
            lo_of_q(0, 1)
            split_low(dve, "wo1", split_lo)
            dve.wait_ge(snap_zeroed, 1)
            dve.wait_ge(ones_ready, 2)

            HI_FIRST = KT_ + LT
            HI = KT_ + LT

            def add_state(c, before, after, step, sem_, inc):
                off = (c % 2) * 2 * AUG
                for h in range(2):
                    rows, cols = slice(h * D, (h + 1) * D), slice(h * AUG, (h + 1) * AUG)
                    last = dve.tensor_tensor(after[rows, cols], kv_bank[rows, off + h * AUG:off + (h + 1) * AUG],
                                             before[rows, cols], ALU.add)
                last.then_inc(sem_, inc)

            def norm(i, p, g):
                v = o_bank[i][:, 0:4 * AUG].rearrange("p (n e) -> p n e", e=AUG)
                n = 2 * p + i
                dve.wait_ge(o_filled, g * (2 * PAIRS) + (n + 1))
                dve.tensor_scalar(den[:, :], v[:, :, D], EPS_ATTN, None, ALU.add).then_inc(den_step, 1)
                dve.wait_ge(den_step, g * (4 * PAIRS) + (2 * n + 1))
                dve.reciprocal(rden[:, :], den[:, :]).then_inc(den_step, 1)
                dve.wait_ge(den_step, g * (4 * PAIRS) + (2 * n + 2))
                dst = o_tok[:, 2 * i:2 * i + 2].rearrange("p c (h e) -> p (c h) e", e=D)
                dve.tensor_tensor(dst, v[:, :, 0:D], rden[:, :].unsqueeze(2).to_broadcast([P, 4, D]), ALU.mult)\
                   .then_inc(o_normed, 1)

            def lo_of_oT(p, g):
                dve.wait_ge(oT_hi, g * PAIRS + (p + 1))
                dve.tensor_tensor(oT[:, 1, p], tr_bank[:, :], oT[:, 0, p].bitcast(F32), ALU.subtract)\
                   .then_inc(oT_ready, 1)

            PHI = 2 * PAIRS

            def unit(p, g):
                if p < PAIRS - 1:
                    phi(f"Q{p + 1}", g * PHI + (2 + 2 * p + 1))
                else:
                    for t in range(KT_):
                        lo_of_work(f"xnT{t}", xnT[:, 1, t], xnT[:, 0, t], g * HI + (HI_FIRST + LT + t + 1))
                dve.wait_ge(kv_filled, g * (2 * PAIRS) + (2 * p + 1))
                add_state(0, state[:, p], snap[:, 0], 0, snap_step, 1)
                dve.wait_ge(snap_step, g * PAIRS + (p + 1))
                add_state(1, snap[:, 0], snap[:, 1], 1, snap_ready, 1)
                if p > 0:
                    lo_of_oT(p - 1, g)
                if p < PAIRS - 1:
                    lo_of_q(p + 1, g * PAIRS + (p + 2))
                dve.wait_ge(kv_filled, g * (2 * PAIRS) + (2 * p + 2))
                dve.wait_ge(snap_ready, g * (2 * PAIRS) + (2 * p + 1))
                add_state(2, snap[:, 1], snap[:, 2], 2, snap_ready, 1)
                if p < PAIRS - 1:
                    phi(f"K{p + 1}", g * PHI + (2 + 2 * p + 2))
                else:
                    values("V0c0", count_of("V0c0", g))
                norm(0, p, g)
                dve.wait_ge(snap_ready, g * (2 * PAIRS) + (2 * p + 2))
                add_state(3, snap[:, 2], state[:, p], 3, state_ready, 1)
                if p < CH:
                    values(f"V1c{p}", count_of(f"V1c{p}", g))
                elif p < CH + LT:
                    t = p - CH
                    lo_of_work(f"leafT{t}", leafT[:, 1, t], leafT[:, 0, t], g * HI + (HI_FIRST + t + 1))
                if p < CH:
                    lo_of_k(p + 1, g * PAIRS + (p + 2))
                norm(1, p, g)
                if CH <= p < PAIRS - 1:
                    lo_of_k(p + 1, g * PAIRS + (p + 2))
                if p == CH:
                    layer_norm(g + 2)
                if p == CH + 1:
                    normalise(g + 2)

            def output(i, name, g):
                dve.wait_ge(y_stored, g * 32 + AHEAD)
                dve.wait_ge(work_filled[bank_of(name)], count_of(name, g))
                dve.tensor_tensor(y_tile[:, 2 * i:2 * i + 2], w(name)[:, :].rearrange("p (c d) -> p c d", d=hid),
                                  resid[:, 2 * i:2 * i + 2], ALU.add)\
                   .then_inc(work_drained[bank_of(name)], 1)

            with dve.Fori(0, batches) as b:
                wait_apart(dve, state_reset, b + 1)
                with dve.Fori(0, MACROS) as m:
                    g = dve.snap(b * MACROS + m)
                    for p in range(PAIRS):
                        unit(p, g)
                    with dve.If(g < final):
                        values("V0c1", count_of("V0c1", g))
                        lo_of_oT(PAIRS - 1, g)
                        for c in range(2, CH):
                            values(f"V0c{c}", count_of(f"V0c{c}", g))
                        for i, kind in enumerate("KQ"):
                            phi(f"{kind}0", g * PHI + (2 + 2 * (PAIRS - 1) + i + 1))
                            (lo_of_k if kind == "K" else lo_of_q)(0, g * PAIRS + (PAIRS + 1))
                            output(i, f"y{i}", g)
            lo_of_oT(PAIRS - 1, final)
            for i in range(2):
                output(i, LAST_Y[i], final)

        @block.tensor
        def _(pe):
            def split_product(dst, lhs, rhs, tiles):
                steps = [s for t in range(tiles) for s in passes(lambda a, t=t: lhs(a, t), lambda a, t=t: rhs(a, t))]
                for i, (l, r) in enumerate(steps):
                    last = pe.matmul(dst, l, r, start=i == 0, stop=i == len(steps) - 1)
                return last

            Y_TILES = list(range(PAIRS, PAIRS + LT)) + list(range(PAIRS))

            def product_y(dst, c, first=0, beyond=PAIRS + LT):
                cols = slice(c * P, (c + 1) * P)
                for n in range(first, beyond):
                    t = Y_TILES[n]
                    for i, (a, b) in enumerate(((0, 0), (0, 1), (1, 0))):
                        end = pe.matmul(dst[:, (c % 2) * hid:(c % 2 + 1) * hid],
                                        oT[:, a, t, cols] if t < PAIRS else leafT[:, a, t - PAIRS, cols],
                                        wo[:, b, t] if t < PAIRS else tree_w[:, b, t - PAIRS],
                                        start=n == 0 and i == 0, stop=n == PAIRS + LT - 1 and i == 2)
                return end

            def fill(name, bank=None):
                dst = work[bank] if bank is not None else w(name)
                if name[0] in "KQ":
                    wt, p = (wk if name[0] == "K" else wq), int(name[1:])
                    return split_product(dst[:, :], lambda a, t: wt[:, a, t, p * P:(p + 1) * P],
                                         lambda a, t: xnT[:, a, t], KT_)
                if name[0] == "V":
                    half, c, n = int(name[1]), int(name[3:]), 2 * HALF * D
                    return split_product(dst[:, 0:n], lambda a, t: xnT[:, a, t, c * P:(c + 1) * P],
                                         lambda a, t: wv[:, a, t, half * n:(half + 1) * n], KT_)
                if name.startswith("xnT") or name.startswith("leafT"):
                    t, src = int(name[-1]), xn if name[0] == "x" else leaf_even
                    for c in range(CH):
                        last = pe.transpose(dst[:, c * P:(c + 1) * P], src[:, c, t * P:(t + 1) * P], ident[:, :])
                    return last
                if name.startswith("gate"):
                    i = int(name[-1])
                    for j in range(2):
                        c = 2 * i + j
                        last = split_product(dst[:, j * leaves:(j + 1) * leaves],
                                             lambda a, t: xnT[:, a, t, c * P:(c + 1) * P],
                                             lambda a, t: route[:, a, t], KT_)
                    return last
                if name.startswith("tree_out"):
                    i = int(name[-1])
                    for t in range(KT_):
                        last = pe.matmul(dst[:, 0:hid], leafvT[:, t, i * P:(i + 1) * P], woutT[:, t],
                                         start=t == 0, stop=t == KT_ - 1)
                    return last
                for c in (2 * int(name[-1]), 2 * int(name[-1]) + 1):
                    last = product_y(dst, c)
                return last

            def first_fill(name):
                i = FIRST_FILLS.index(name)
                if i >= 2:
                    pe.wait_ge(work_drained[i % 2], i // 2)
                fill(name, i % 2).then_inc(work_filled[i % 2], 1)

            def loop_fill(name, g):
                pe.wait_ge(work_drained[bank_of(name)], g * PER_BANK + (FIRST_PER_BANK + FILLS.index(name) // 2))
                fill(name).then_inc(work_filled[bank_of(name)], 1)

            pe.wait_ge(ident_ready, 1)
            pe.wait_ge(loaded["bias"], 32)
            pe.transpose(tr_bank[:, 0:2 * PAIRS], bias_rows[:, :], ident[0:2 * PAIRS, 0:2 * PAIRS])\
              .then_inc(biasT_filled, 1)
            pe.wait_ge(loaded["small"], 80)
            for src, dst in ((routers_in, s_bank[0]), (leaf_in, s_bank[1]), (wout_in, o_bank[0])):
                v = dst[:, :].rearrange("p (t n) -> p t n", t=2)
                for i in range(2):
                    for j in range(2):
                        last = pe.transpose(v[:, i, j * P:(j + 1) * P], src[:, j, i * P:(i + 1) * P], ident[:, :])
                last.then_inc(treeT_filled, 1)
            pe.wait_ge(xn_ready, 1)
            first_fill("xnT0")
            first_fill("xnT1")
            pe.wait_ge(treeT_ready, 1)
            for i in range(KT_):
                for t in range(KT_):
                    last = pe.matmul(kv_bank[:, i * leaves:(i + 1) * leaves], tree_wq_in[:, t, i * P:(i + 1) * P],
                                     routersT[:, t], start=t == 0, stop=t == KT_ - 1)
            last.then_inc(route_filled, 1)
            pe.wait_ge(split_lo, LO_VECTOR.index("wv0") + 1)
            pe.wait_ge(work_drained[1], 1)
            first_fill("V0c0")
            first_fill("V0c1")
            pe.wait_ge(treeT_ready, 3)
            first_fill("tree_out0")
            first_fill("V0c2")
            pe.wait_ge(split_lo, LO_VECTOR.index("wk0") + 1)
            first_fill("K0")
            first_fill("V0c3")
            pe.wait_ge(split_lo, LO_VECTOR.index("wq0") + 1)
            first_fill("Q0")
            first_fill("tree_out1")
            pe.wait_ge(route_ready, 1)
            first_fill("gate0")
            first_fill("gate1")
            pe.wait_ge(split_lo_pool, len(LO_POOL))
            pe.wait_ge(ones_ready, 2)

            def transpose_o(p, g):
                pe.wait_ge(o_normed, g * (2 * PAIRS) + (AHEAD + 2 * p + 2))
                pe.wait_ge(k_tok_ready, g * PAIRS + min(p + 2, PAIRS))
                for c in range(CH):
                    last = pe.transpose(tr_bank[:, c * P:(c + 1) * P], o_tok[:, c], ident[:, :])
                last.then_inc(o_tr_filled, 1)

            def outer_products(i, p, g):
                half, off = p // HALF, (p % HALF) * 2 * AUG
                for c in (2 * i, 2 * i + 1):
                    last = pe.matmul(kv_bank[:, (c % 2) * 2 * AUG:(c % 2 + 1) * 2 * AUG], k_tok[:, c],
                                     v_aug[:, half, c, off:off + 2 * AUG], start=True, stop=True)
                last.then_inc(kv_filled, 1)

            def attend(i, p, g):
                half = p // HALF
                for c in (2 * i, 2 * i + 1):
                    at = (c % 2) * 2 * AUG
                    before = state[:, p] if c == 0 else snap[:, c - 1]
                    pe.matmul(o_bank[i][:, at:at + 2 * AUG], qT[:, p % 2, c * P:(c + 1) * P], before,
                              start=True, stop=False)
                    for h in range(2):
                        off = (2 * (p % HALF) + h) * AUG
                        last = pe.matmul(o_bank[i][:, at + h * AUG:at + (h + 1) * AUG], aT[:, c, h],
                                         v_aug[:, half, c, off:off + AUG], start=False, stop=h == 1)
                last.then_inc(o_filled, 1)

            def unit(p, g):
                if p == 0:
                    pe.wait_ge(work_drained[bank_of("K0")], count_before("K0", g))
                    pe.wait_ge(oT_ready, g * PAIRS + AHEAD)
                elif p == 1:
                    pe.wait_ge(work_drained[bank_of("K1")], count_of("K1", g))
                    pe.wait_ge(k_tok_ready, g * PAIRS + 1)
                else:
                    pe.wait_ge(work_drained[bank_of(f"K{p}")], count_of(f"K{p}", g))
                    pe.wait_ge(oT_ready, g * PAIRS + (AHEAD + p - 1))
                for c in range(CH):
                    last = pe.transpose(tr_bank[:, c * P:(c + 1) * P], kT[:, p % 2, c * P:(c + 1) * P], ident[:, :])
                last.then_inc(k_tr_filled, 1)
                if p < PAIRS - 1:
                    loop_fill(f"Q{p + 1}", g)
                else:
                    pe.wait_ge(xn_ready, g + 2)
                    loop_fill("xnT0", g)
                    loop_fill("xnT1", g)
                if p > 0:
                    transpose_o(p - 1, g)
                pe.wait_ge(k_split_ready, g * PAIRS + (p + 1))
                pe.wait_ge(q_split_ready, g * PAIRS + (p + 1))
                if p in SHARED:
                    pe.wait_ge(q_low_ready, g * len(SHARED) + (SHARED.index(p) + 1))
                pe.wait_ge(s_copied, g * (2 * PAIRS) + (AHEAD + 2 * p))
                for c in range(CH):
                    if c == CH // 2 and p in SHARED:
                        pe.wait_ge(k_low_ready, g * len(SHARED) + (SHARED.index(p) + 1))
                    at = (c % 2) * 2 * P
                    last = split_product(s_bank[c // 2][:, at:at + 2 * P],
                                         lambda a, t: k_split[:, a, c * P:(c + 1) * P],
                                         lambda a, t: q_split[:, a, c].rearrange("p h n -> p (h n)"), 1)
                    if c % 2:
                        last.then_inc(s_filled, 1)
                if p == HALF:
                    pe.wait_ge(work_drained[bank_of("V1c3")], count_of("V1c3", g))
                    pe.wait_ge(work_drained[bank_of("V1c2")], count_of("V1c2", g))
                pe.wait_ge(k_tok_ready, g * PAIRS + (p + 1))
                pe.wait_ge(state_ready, g * PAIRS + (AHEAD + p))
                outer_products(0, p, g)
                if p < PAIRS - 1:
                    loop_fill(f"K{p + 1}", g)
                else:
                    for t in range(KT_):
                        pe.wait_ge(work_drained[bank_of(f"xnT{t}")], count_of(f"xnT{t}", g))
                    loop_fill("V0c0", g)
                pe.wait_ge(snap_ready, g * (2 * PAIRS) + (2 * p + 1))
                outer_products(1, p, g)
                pe.wait_ge(a_masked, g * (2 * PAIRS) + (2 * p + 1))
                pe.wait_ge(o_normed, g * (2 * PAIRS) + (AHEAD + 2 * p))
                attend(0, p, g)
                if p < CH:
                    loop_fill(f"V1c{p}", g)
                elif p < CH + LT:
                    if p == CH:
                        pe.wait_ge(leaf_step, (g + 1) * (2 * depth + 1))
                    loop_fill(f"leafT{p - CH}", g)
                pe.wait_ge(a_masked, g * (2 * PAIRS) + (2 * p + 2))
                pe.wait_ge(snap_ready, g * (2 * PAIRS) + (2 * p + 2))
                attend(1, p, g)

            with pe.Fori(0, batches) as b:
                wait_apart(pe, state_reset, b + 1)
                with pe.Fori(0, MACROS) as m:
                    g = pe.snap(b * MACROS + m)
                    for p in range(PAIRS):
                        unit(p, g)
                    with pe.If(g < final):
                        loop_fill("V0c1", g)
                        transpose_o(PAIRS - 1, g)
                        for name in ("V0c2", "V0c3", "K0"):
                            loop_fill(name, g)
                        pe.wait_ge(oT_ready, g * PAIRS + (AHEAD + PAIRS))
                        pe.wait_ge(split_lo, len(LO_VECTOR))
                        for name in ("y0", "Q0", "y1", "gate0", "gate1"):
                            loop_fill(name, g)

            pe.wait_ge(oT_ready, final * PAIRS + (AHEAD + PAIRS - 1))
            y_banks = [w(name) for name in LAST_Y]
            pe.wait_ge(work_drained[bank_of(LAST_Y[0])], count_of(LAST_Y[0], final) - 1)
            product_y(y_banks[0], 0, 0, HALF)
            transpose_o(PAIRS - 1, final)
            product_y(y_banks[0], 0, HALF, PAIRS + LT - 1)
            pe.wait_ge(oT_ready, final * PAIRS + (AHEAD + PAIRS))
            product_y(y_banks[0], 0, PAIRS + LT - 1)
            product_y(y_banks[0], 1).then_inc(work_filled[bank_of(LAST_Y[0])], 1)
            pe.wait_ge(work_drained[bank_of(LAST_Y[1])], count_of(LAST_Y[1], final) - 1)
            product_y(y_banks[1], 2)
            product_y(y_banks[1], 3).then_inc(work_filled[bank_of(LAST_Y[1])], 1)


_INS = ['L0_attn_x', 'L0_attn_Wq', 'L0_attn_bq', 'L0_attn_Wk', 'L0_attn_bk', 'L0_attn_Wv', 'L0_attn_bv',
        'L0_attn_Wo', 'L0_attn_bo', 'L0_ffn_Wq', 'L0_ffn_routers', 'L0_ffn_leaf_keys', 'L0_ffn_leaf_values',
        'L0_ffn_Wout_w', 'L0_ffn_Wout_b']


def kernel(**inputs):
    import numpy as _np
    import concourse.bacc as _bacc
    from concourse import mybir as _mybir
    from concourse.bass_utils import run_bass_kernel_spmd as _run

    nc = _bacc.Bacc("TRN2", target_bir_lowering=False, num_devices=1)
    arrays, args = {}, []
    for name in _INS:
        a = _np.ascontiguousarray(inputs[name])
        arrays[f"in_{name}_dram"] = a
        args.append(nc.dram_tensor(f"in_{name}_dram", a.shape, _mybir.dt.from_np(a.dtype), kind="ExternalInput").ap())
    shape = inputs['L0_attn_x'].shape
    out = nc.dram_tensor("out_dram", shape, _mybir.dt.float32, kind="ExternalOutput").ap()
    attention_and_tree_layer(nc, *args, out)
    r = _run(nc, [arrays], core_ids=[0])
    return r.results[0]["out_dram"]
```
